# Optimizing a Trainium2 kernel written in Bass

```python
import numpy as np
import jax
import jax.numpy as jnp

def _softmax(x, axis=-1):
    return jax.nn.softmax(x, axis=axis)

def _gelu(x):
    return jax.nn.gelu(x, approximate=True)

def _silu(x):
    return jax.nn.silu(x)

def _sigmoid(x):
    return jax.nn.sigmoid(x)

def _layernorm(x, axis=-1, eps=1e-05):
    m = jnp.mean(x, axis=axis, keepdims=True)
    v = jnp.var(x, axis=axis, keepdims=True)
    return (x - m) / jnp.sqrt(v + eps)

def _scatter_add(tgt, idx, src, axis=0):
    return tgt.at[idx].add(src)

def _segment_sum(src, seg, n):
    return jax.ops.segment_sum(src, seg, n)
kernel_name = 'mk_seq_postln_d1_jaxref_r4_2717a1'

def setup_inputs(seed: int=0):
    np.random.seed(seed)
    _w = jnp.asarray

    def _L0_attn_setup():
        import jax, jax.numpy as jnp
        import numpy as np
        HIDDEN = 256
        HEADS = 16
        HEAD_DIM = HIDDEN // HEADS
        ROPE_BASE = 10000.0

        def _rope_cos_sin(seq_len, dim):
            inv_freq = 1.0 / ROPE_BASE ** (jnp.arange(0, dim, 2, dtype=jnp.float32) / dim)
            t = jnp.arange(seq_len, dtype=jnp.float32)
            freqs = jnp.einsum('i,j->ij', t, inv_freq)
            emb = jnp.concatenate([freqs, freqs], axis=-1)
            return (jnp.cos(emb), jnp.sin(emb))

        def _apply_rope(x, cos, sin):
            x1, x2 = (x[..., 0::2], x[..., 1::2])
            c = cos[..., :x1.shape[-1]]
            s = sin[..., :x1.shape[-1]]
            return jnp.concatenate([x1 * c - x2 * s, x1 * s + x2 * c], axis=-1)
        key = jax.random.key(seed)
        ks = jax.random.split(key, 9)
        B, S = (4, 512)
        lim = 1.0 / np.sqrt(HIDDEN)

        def lin(kw, kb):
            W = jax.random.uniform(kw, (HIDDEN, HIDDEN), jnp.float32, -lim, lim)
            b = jax.random.uniform(kb, (HIDDEN,), jnp.float32, -lim, lim)
            return (W, b)
        Wq, bq = lin(ks[0], ks[1])
        Wk, bk = lin(ks[2], ks[3])
        Wv, bv = lin(ks[4], ks[5])
        Wo, bo = lin(ks[6], ks[7])
        x = jax.random.normal(ks[8], (B, S, HIDDEN), jnp.float32)
        return {'x': x, 'Wq': Wq, 'bq': bq, 'Wk': Wk, 'bk': bk, 'Wv': Wv, 'bv': bv, 'Wo': Wo, 'bo': bo}
    _L0_attn_in = _L0_attn_setup()

    def _L0_ffn_setup():
        import jax, jax.numpy as jnp
        import numpy as np
        EPS = 1e-05

        def _quantize(W):
            gamma = jnp.mean(jnp.abs(W))
            return jnp.clip(jnp.round(W / (gamma + EPS)), -1.0, 1.0)
        key = jax.random.key(seed)
        k_x, k_w1, k_b1, k_w2, k_b2 = jax.random.split(key, 5)
        n_embd = 256
        d_ff = 4 * n_embd
        B, S = (4, 1024)
        bound1 = 1.0 / np.sqrt(n_embd)
        bound2 = 1.0 / np.sqrt(d_ff)
        x = jax.random.normal(k_x, (B, S, n_embd), dtype=jnp.float32)
        W1 = jax.random.uniform(k_w1, (d_ff, n_embd), jnp.float32, -bound1, bound1)
        b1 = jax.random.uniform(k_b1, (d_ff,), jnp.float32, -bound1, bound1)
        W2 = jax.random.uniform(k_w2, (n_embd, d_ff), jnp.float32, -bound2, bound2)
        b2 = jax.random.uniform(k_b2, (n_embd,), jnp.float32, -bound2, bound2)
        return {'x': x, 'W1': W1, 'b1': b1, 'W2': W2, 'b2': b2}
    _L0_ffn_in = _L0_ffn_setup()
    _d = {'L0_attn_x': _L0_attn_in['x'], 'L0_attn_Wq': _L0_attn_in['Wq'], 'L0_attn_bq': _L0_attn_in['bq'], 'L0_attn_Wk': _L0_attn_in['Wk'], 'L0_attn_bk': _L0_attn_in['bk'], 'L0_attn_Wv': _L0_attn_in['Wv'], 'L0_attn_bv': _L0_attn_in['bv'], 'L0_attn_Wo': _L0_attn_in['Wo'], 'L0_attn_bo': _L0_attn_in['bo'], 'L0_ffn_W1': _L0_ffn_in['W1'], 'L0_ffn_b1': _L0_ffn_in['b1'], 'L0_ffn_W2': _L0_ffn_in['W2'], 'L0_ffn_b2': _L0_ffn_in['b2']}
    _x0 = _d['L0_attn_x']
    _d['L0_attn_x'] = jax.random.normal(jax.random.fold_in(jax.random.key(seed), 1), (16, 1024, 256), dtype=_x0.dtype)
    del _x0
    return _d

def reference(L0_attn_x, L0_attn_Wq, L0_attn_bq, L0_attn_Wk, L0_attn_bk, L0_attn_Wv, L0_attn_bv, L0_attn_Wo, L0_attn_bo, L0_ffn_W1, L0_ffn_b1, L0_ffn_W2, L0_ffn_b2):

    def _L0_attn_ref(x, Wq, bq, Wk, bk, Wv, bv, Wo, bo):
        import jax, jax.numpy as jnp
        import numpy as np
        HIDDEN = 256
        HEADS = 16
        HEAD_DIM = HIDDEN // HEADS
        ROPE_BASE = 10000.0

        def _rope_cos_sin(seq_len, dim):
            inv_freq = 1.0 / ROPE_BASE ** (jnp.arange(0, dim, 2, dtype=jnp.float32) / dim)
            t = jnp.arange(seq_len, dtype=jnp.float32)
            freqs = jnp.einsum('i,j->ij', t, inv_freq)
            emb = jnp.concatenate([freqs, freqs], axis=-1)
            return (jnp.cos(emb), jnp.sin(emb))

        def _apply_rope(x, cos, sin):
            x1, x2 = (x[..., 0::2], x[..., 1::2])
            c = cos[..., :x1.shape[-1]]
            s = sin[..., :x1.shape[-1]]
            return jnp.concatenate([x1 * c - x2 * s, x1 * s + x2 * c], axis=-1)
        B, S, _ = x.shape
        scale = HEAD_DIM ** (-0.5)

        def proj(W, b):
            y = jnp.einsum('bsd,ed->bse', x, W) + b
            return y.reshape(B, S, HEADS, HEAD_DIM).transpose(0, 2, 1, 3)
        q = proj(Wq, bq)
        k = proj(Wk, bk)
        v = proj(Wv, bv)
        cos, sin = _rope_cos_sin(S, HEAD_DIM)
        cos = cos[None, None]
        sin = sin[None, None]
        q = _apply_rope(q, cos, sin) * scale
        k = _apply_rope(k, cos, sin)
        attn = jnp.einsum('bhsd,bhtd->bhst', q, k)
        attn = jax.nn.softmax(attn, axis=-1)
        out = jnp.einsum('bhst,bhtd->bhsd', attn, v)
        out = out.transpose(0, 2, 1, 3).reshape(B, S, HIDDEN)
        return jnp.einsum('bsd,ed->bse', out, Wo) + bo

    def _L0_ffn_ref(x, W1, b1, W2, b2):
        import jax, jax.numpy as jnp
        import numpy as np
        EPS = 1e-05

        def _quantize(W):
            gamma = jnp.mean(jnp.abs(W))
            return jnp.clip(jnp.round(W / (gamma + EPS)), -1.0, 1.0)
        Wq1 = _quantize(W1)
        Wq2 = _quantize(W2)
        h = jax.nn.relu(jnp.einsum('bsd,fd->bsf', x, Wq1) + b1)
        out = jnp.einsum('bsf,df->bsd', h, Wq2) + b2
        return out
    x = L0_attn_x
    x = _layernorm(x + _L0_attn_ref(x, L0_attn_Wq, L0_attn_bq, L0_attn_Wk, L0_attn_bk, L0_attn_Wv, L0_attn_bv, L0_attn_Wo, L0_attn_bo), axis=-1)
    x = _layernorm(x + _L0_ffn_ref(x, L0_ffn_W1, L0_ffn_b1, L0_ffn_W2, L0_ffn_b2), axis=-1)
    return x

_drawn_inputs = setup_inputs


def setup_inputs(seed=0):
    import zlib

    import numpy as np

    out = dict(_drawn_inputs(seed))
    spreads = {}
    factors = {'L0_attn_Wq': 8.0,
     'L0_attn_bq': 8.0,
     'L0_attn_Wk': 8.0,
     'L0_attn_bk': 8.0,
     'L0_attn_Wv': 4.871,
     'L0_ffn_b1': 21.642,
     'L0_ffn_b2': 64.0,
     'L0_attn_bv': 4.683,
     'L0_attn_bo': 2.807}
    for name, (base, spread) in spreads.items():
        noise = np.random.default_rng([zlib.crc32(name.encode()), seed]).standard_normal(out[name].shape)
        drawn = base * np.exp(spread * noise) if base else spread * noise
        out[name] = jnp.asarray(drawn.astype(out[name].dtype))
    for name, factor in factors.items():
        out[name] = (out[name] * factor).astype(out[name].dtype)
    return out
```

```python
import numpy as np

import concourse.bass as bass
from concourse import mybir
from contextlib import ExitStack

B, S, D = 16, 1024, 256
H, HD = 16, 16
F = 1024
P = 128
G = 4
HG = H // G
TQ = S // G
TL = TQ // P
TT = S // P
KC = D // P
FT = F // P
QH = 2
NQ = S // QH
STEPS = QH * TT
LEAD = 2
VW = HD + 1
PARTS = 3
TERMS = 6
ROWS = TERMS * HD
MROWS = 2
Q_PARTS = [0, 0, 1, 1, 0, 2]
K_PARTS = [0, 1, 0, 1, 2, 0]
EPS = 1e-5
NS1 = HG * TT * 2
MAX_STEPS = 12

STEP_OF = {"e": 1, "o": 2, "v": 3, "t1a": 4, "t1b": 5, "t2": 6, "t3": 7, "t4": 9,
           "f0": 10, "f1": 11, "mx": 12, "f2": 12, "f3": 13, "t6a": 14, "t6b": 15}


def maximum_tiles(s):
    if s >= MAX_STEPS:
        return range(0, 0)
    return range(NS1 * s // MAX_STEPS, NS1 * (s + 1) // MAX_STEPS)


def wait_used(engine, semaphore, count):
    if not isinstance(count, int) or count > 0:
        engine.wait_ge(semaphore, count)


def build(nc, x, xt, wqk, bqk, wv, bv, wo, bo, w1, b1, w2, b2, rope, ident, out):
    fp32 = mybir.dt.float32
    bf16 = mybir.dt.bfloat16
    ALU = mybir.AluOpType
    ACT = mybir.ActivationFunctionType
    AX = mybir.AxisListType

    qk_d = nc.dram_tensor("qk_parts", (B, 2, D, PARTS, S), bf16).ap()
    v_d = nc.dram_tensor("v_ones", (B, G, P, TT * HG * VW), fp32).ap()
    at_d = nc.dram_tensor("attention", (B, G, P, S), fp32).ap()
    m_d = nc.dram_tensor("maxima", (B, G, MROWS, HG * S), bf16).ap()

    with ExitStack() as ctx:
        def sb(name, shape, dt=fp32):
            return ctx.enter_context(nc.sbuf_tensor(name, shape, dt))

        def pb(name, shape):
            return ctx.enter_context(nc.psum_tensor(name, shape, fp32))

        def sem(name):
            return ctx.enter_context(nc.semaphore(name))

        id_sb = sb("id_sb", [P, P])
        ones = sb("ones", [P, P])
        wqk_sb = sb("wqk_sb", [P, KC, 2, 2, P])
        bqk_sb = sb("bqk_sb", [P, 2, 2])
        wv_sb = sb("wv_sb", [P, KC, D])
        wo_sb = sb("wo_sb", [P, KC, D])
        w1_sb = sb("w1_sb", [P, KC, F])
        w2_sb = sb("w2_sb", [P, FT, D])
        b1_sb = sb("b1_sb", [P, FT])
        bv_sb = sb("bv_sb", [P, D])
        bo_sb = sb("bo_sb", [P, D])
        b2_sb = sb("b2_sb", [P, D])
        cs_sb = sb("cs_sb", [P, 2, 2, S])
        half_sb = sb("half_sb", [P, TL])
        asum = sb("asum", [P, 2])
        thr = sb("thr", [P, 2, 2])

        xt_sb = sb("xt_sb", [P, KC, TQ])
        ev_sb = sb("ev_sb", [P, 2, TQ])
        od_sb = sb("od_sb", [P, 2, TQ])
        ec = sb("ec", [P, 2, TQ])
        os_ = sb("os_", [P, 2, TQ])
        es = sb("es", [P, 2, TQ])
        oc = sb("oc", [P, 2, TQ])
        rot = sb("rot", [P, 2, 2, TQ])
        rest = sb("rest", [P, 2, 2, TQ])
        parts = sb("parts", [P, 2, 2, PARTS, TQ], bf16)
        v_st = sb("v_st", [P, G, TL, HG, VW])

        qa = [sb(f"qa{i}", [P, HG, S], bf16) for i in range(G)]
        ka = [sb(f"ka{i}", [P, HG, S], bf16) for i in range(G)]
        v_sb = [sb(f"v_sb{i}", [P, TT, HG, VW]) for i in range(2)]
        prob = [sb(f"prob{i}", [P, HG, NQ]) for i in range(2)]
        at_st = [sb(f"at_st{i}", [P, NQ]) for i in range(QH)]
        mxp = sb("mxp", [P, 2, HG * TT])
        mx = sb("mx", [P, HG * TT])
        nm = sb("nm", [HG * TT, MROWS, P], bf16)

        at_sb = sb("at_sb", [P, G, TQ])
        rden = sb("rden", [P, TL, H])
        att = sb("att", [P, TL, D])
        att_t = sb("att_t", [P, KC, TQ])
        xn = sb("xn", [P, TL, D])
        xb = sb("xb", [P, TL, D])
        y = sb("y", [P, TL, D])
        st = sb("st", [P, TL, 6])
        mv = sb("mv", [P, TL, 2])
        ve = sb("ve", [P, TL])
        rstd = sb("rstd", [P, TL])
        h1 = sb("h1", [P, TL, D])
        h1b = sb("h1b", [P, TL, D])
        h1_t = sb("h1_t", [P, KC, TQ])
        hid = sb("hid", [P, FT, TQ])
        y2 = sb("y2", [P, TL, D])
        st2 = sb("st2", [P, TL, 6])
        mv2 = sb("mv2", [P, TL, 2])
        ve2 = sb("ve2", [P, TL])
        rstd2 = sb("rstd2", [P, TL])
        res = sb("res", [P, TL, D])

        sc = [pb(f"sc{i}", [P, 2, NQ]) for i in range(2)]
        ms = [pb(f"ms{i}", [P, 512]) for i in range(2)]
        ob = pb("ob", [P, NQ])
        job = pb("job", [P, 512])

        names = """consts_loaded w1_loaded w2_loaded abs_summed sums_ready thresholds_set thr_half signs_done ternary_done
            ones_set powers_set xt_loaded even_ready even_taken odd_ready odd_taken v_ready v_taken roped products
            rotated rest_done mid_done parts_done parts_stored v_stored
            m_stored m_loaded s1_ready s1_taken max_done mx_ready high_done mx_taken
            s2_ready exp_done pv_done o_taken ob_zero
            at_loaded t1_ready recip_done t1_taken t2_ready t2_taken t3_ready t3_taken y_done stats_done moments_done
            var_done rstd_done h1_done t4_ready t4_taken f_ready f_taken t6_ready t6_taken
            xn_loaded xb_done h1b_done y2_done stats2_done moments2_done var2_done rstd2_done res_done out_stored""".split()
        s = {n: sem(n) for n in names}
        qk_loaded = [sem(f"qk_loaded{i}") for i in range(G)]
        v_loaded = [sem(f"v_loaded{i}") for i in range(2)]
        at_stored = [sem(f"at_stored{i}") for i in range(QH)]

        def upto(b, g, each, n):
            return b * (G * each) + (g * each + n)

        block = ctx.enter_context(nc.Block())
        QK_DMAS = 2 * TERMS

        @block.sync
        def _(sp):
            def proj_in(b, g):
                wait_used(sp, s["v_ready"], upto(b, g, 1, 0))
                sp.dma_start(xt_sb[:, :, :], xt[b].rearrange("(c p) t -> p c t", p=P)[:, :, g * TQ:(g + 1) * TQ]
                             ).then_inc(s["xt_loaded"], 16)

            def proj_out(b, g):
                sp.wait_ge(s["v_taken"], upto(b, g, 1, 1))
                for tl in range(1):
                    sp.dma_start(v_d[b].rearrange("g p n -> p g n")[:, :, g * TL * HG * VW:(g + 1) * TL * HG * VW],
                                 v_st[:, :, :, :, :].rearrange("p g t h c -> p g (t h c)")).then_inc(s["v_stored"], 16)
                sp.wait_ge(s["parts_done"], upto(b, g, 1, 1))
                for i in range(2):
                    sp.dma_start(
                        qk_d[b, i].rearrange("(p e) a t -> p (e a) t", e=2)[:, :, g * TQ:(g + 1) * TQ],
                        parts[:, i].rearrange("p e a t -> p (e a) t")).then_inc(s["parts_stored"], 16)

            def load_qk(b, g):
                sp.wait_ge(s["parts_stored"], upto(b, G, 32, 0))
                for i, (dst, order) in enumerate(((qa[g], Q_PARTS), (ka[g], K_PARTS))):
                    rows = qk_d[b, i, g * HG * HD:(g + 1) * HG * HD].rearrange("(h r) a t -> a r h t", r=HD)
                    for n, a in enumerate(order):
                        sp.dma_start(dst[n * HD:(n + 1) * HD, :, :], rows[a]).then_inc(qk_loaded[g], 16)

            def load_v(b, g):
                sp.wait_ge(s["v_stored"], upto(b, G, 16, 0))
                sp.dma_start(v_sb[g % 2][:, :, :, :].rearrange("p t h c -> p (t h c)"), v_d[b, g]
                             ).then_inc(v_loaded[g % 2], 16)

            def move_maxima(b, g):
                sp.wait_ge(s["mx_taken"], upto(b, g, 1, 1))
                sp.dma_start(m_d[b, g].rearrange("m (r c) -> r m c", c=P), nm[:, :, :]).then_inc(s["m_stored"], 16)
                sp.wait_ge(s["m_stored"], upto(b, g, 16, 16))
                sp.dma_start(qa[g][ROWS:ROWS + MROWS, :, :].rearrange("p h t -> p (h t)"), m_d[b, g]
                             ).then_inc(s["m_loaded"], 16)

            def store_attention(b, g, qh):
                sp.wait_ge(s["o_taken"], upto(b, g, QH, qh + 1))
                sp.dma_start(at_d[b, g, :, qh * NQ:(qh + 1) * NQ], at_st[qh][:, :]).then_inc(at_stored[qh], 16)

            def tail_in(b, g):
                wait_used(sp, s["xb_done"], upto(b, g, 1, 0))
                for qh in range(QH):
                    sp.wait_ge(at_stored[qh], upto(b, G, 16, 0))
                wait_used(sp, s["t1_ready"], upto(b, g, TL, 0))
                sp.dma_start(xn[:, :, :], x[b, g * TQ:(g + 1) * TQ].rearrange("(t p) f -> p t f", p=P)
                             ).then_inc(s["xn_loaded"], 16)
                sp.dma_start(at_sb[:, :, :], at_d[b].rearrange("g p t -> p g t")[:, :, g * TQ:(g + 1) * TQ]
                             ).then_inc(s["at_loaded"], 16)

            def tail_out(b, g):
                sp.wait_ge(s["res_done"], upto(b, g, TL, TL))
                sp.dma_start(out[b, g * TQ:(g + 1) * TQ].rearrange("(t p) f -> p t f", p=P), res[:, :, :]
                             ).then_inc(s["out_stored"], 16)

            def unit(b, g, proj, tail, last, first):
                after_first = not (first and g == 0)
                if not (last and g >= 2):
                    load_qk(b + (g + 2) // G, (g + 2) % G)
                if proj:
                    proj_in(b + LEAD, g)
                if after_first:
                    store_attention(b + (g - 1) // G, (g - 1) % G, 1)
                if not (last and g == G - 1):
                    load_v(b + (g + 1) // G, (g + 1) % G)
                if tail:
                    tail_in(b - 1, g)
                if proj:
                    proj_out(b + LEAD, g)
                store_attention(b, g, 0)
                if not (last and g == G - 1):
                    move_maxima(b + (g + 1) // G, (g + 1) % G)
                if tail:
                    tail_out(b - 1, g)

            def batch(b, proj=True, tail=True, last=False, first=False):
                for g in range(G):
                    unit(b, g, proj, tail, last, first)

            sp.dma_start(wqk_sb[:, :, :, :, :], wqk).then_inc(s["consts_loaded"], 16)
            sp.dma_start(bqk_sb[:, :, :], bqk).then_inc(s["consts_loaded"], 16)
            sp.dma_start(wv_sb[:, :, :], wv.rearrange("(c p) f -> p c f", p=P)).then_inc(s["consts_loaded"], 16)
            sp.dma_start(cs_sb[:, :, :, :], rope).then_inc(s["consts_loaded"], 16)
            sp.dma_start(bv_sb[:, :], bv.partition_broadcast(P)).then_inc(s["consts_loaded"], 16)
            sp.dma_start(id_sb[:, :], ident).then_inc(s["consts_loaded"], 16)
            sp.dma_start(wo_sb[:, :, :], wo.rearrange("(c p) f -> p c f", p=P)).then_inc(s["consts_loaded"], 16)
            sp.dma_start(bo_sb[:, :], bo.partition_broadcast(P)).then_inc(s["consts_loaded"], 16)
            sp.dma_start(b2_sb[:, :], b2.partition_broadcast(P)).then_inc(s["consts_loaded"], 16)
            sp.dma_start(b1_sb[:, :], b1).then_inc(s["consts_loaded"], 16)
            sp.dma_start(w1_sb[:, :, :], w1.rearrange("(c p) f -> p c f", p=P)).then_inc(s["w1_loaded"], 16)
            sp.dma_start(w2_sb[:, :, :], w2.rearrange("(c p) f -> p c f", p=P)).then_inc(s["w2_loaded"], 16)
            for b in range(LEAD):
                for g in range(G):
                    proj_in(b, g)
                    proj_out(b, g)
            load_qk(0, 0)
            load_qk(0, 1)
            load_v(0, 0)
            move_maxima(0, 0)
            batch(0, tail=False, first=True)
            batch(1)
            with sp.Fori(2, B - LEAD) as b:
                batch(b)
            batch(B - 2, proj=False)
            batch(B - 1, proj=False, last=True)
            store_attention(B - 1, G - 1, 1)
            for g in range(G):
                tail_in(B - 1, g)
                tail_out(B - 1, g)
            sp.wait_ge(s["out_stored"], 16 * B * G)

        @block.tensor
        def _(pe):
            def proj_job(b, g, name, bank_free):
                if name == "e":
                    pe.wait_ge(s["xt_loaded"], upto(b, g, 16, 16))
                for what, n in bank_free:
                    wait_used(pe, s[what], n)
                if name == "v":
                    for tl in range(TL):
                        for c in range(KC):
                            last = nc.tensor.matmul(job[:, tl * D:(tl + 1) * D], xt_sb[:, c, tl * P:(tl + 1) * P],
                                                    wv_sb[:, c, :], start=(c == 0), stop=(c == KC - 1))
                    last.then_inc(s["v_ready"], 1)
                    return [("v_taken", upto(b, g, 1, 1))]
                eo = "eo".index(name)
                for i in range(2):
                    for c in range(KC):
                        last = nc.tensor.matmul(job[:, i * TQ:(i + 1) * TQ], wqk_sb[:, c, i, eo, :], xt_sb[:, c, :],
                                                start=(c == 0), stop=(c == KC - 1))
                name = ("even", "odd")[eo]
                last.then_inc(s[name + "_ready"], 1)
                return [(name + "_taken", upto(b, g, 1, 1))]

            def tail_job(b, g, name, bank_free):
                if name == "t1a":
                    pe.wait_ge(s["at_loaded"], upto(b, g, 16, 16))
                elif name == "t2":
                    pe.wait_ge(s["t1_taken"], upto(b, g, TL, TL))
                elif name == "t3":
                    pe.wait_ge(s["t2_taken"], upto(b, g, 1, 1))
                elif name == "t4":
                    pe.wait_ge(s["h1_done"], upto(b, g, TL, TL))
                elif name == "f0":
                    pe.wait_ge(s["t4_taken"], upto(b, g, 1, 1))
                elif name == "t6a":
                    pe.wait_ge(s["f_taken"], upto(b, g, FT, FT))
                if name != "t6b":
                    for what, n in bank_free:
                        wait_used(pe, s[what], n)
                if name in ("t1a", "t1b"):
                    tl = "ab".index(name[-1])
                    for gg in range(G):
                        last = nc.tensor.transpose(job[:, gg * P:(gg + 1) * P], at_sb[:, gg, tl * P:(tl + 1) * P],
                                                   id_sb[:, :])
                    last.then_inc(s["t1_ready"], 1)
                    return [("t1_taken", upto(b, g, TL, tl + 1))]
                if name in ("t2", "t4"):
                    src = {"t2": att, "t4": h1}[name]
                    for c in range(KC):
                        for tl in range(TL):
                            last = nc.tensor.transpose(job[:, c * TQ + tl * P:c * TQ + (tl + 1) * P],
                                                       src[:, tl, c * P:(c + 1) * P], id_sb[:, :])
                    last.then_inc(s[name + "_ready"], 1)
                    return [(name + "_taken", upto(b, g, 1, 1))]
                if name == "t3":
                    for tl in range(TL):
                        for c in range(KC):
                            last = nc.tensor.matmul(job[:, tl * D:(tl + 1) * D], att_t[:, c, tl * P:(tl + 1) * P],
                                                    wo_sb[:, c, :], start=(c == 0), stop=(c == KC - 1))
                    last.then_inc(s["t3_ready"], 1)
                    return [("t3_taken", upto(b, g, 1, 1))]
                if name[0] == "f":
                    n = int(name[1])
                    for i in range(2):
                        f = 2 * n + i
                        for c in range(KC):
                            last = nc.tensor.matmul(job[:, i * TQ:(i + 1) * TQ], w1_sb[:, c, f * P:(f + 1) * P],
                                                    h1_t[:, c, :], start=(c == 0), stop=(c == KC - 1))
                    last.then_inc(s["f_ready"], 1)
                    return [("f_taken", upto(b, g, FT, 2 * n + 2))]
                tl = "ab".index(name[-1])
                for f in range(FT):
                    last = nc.tensor.matmul(job[:, tl * D:(tl + 1) * D], hid[:, f, tl * P:(tl + 1) * P],
                                            w2_sb[:, f, :], start=(f == 0), stop=(f == FT - 1))
                if name == "t6b":
                    last.then_inc(s["t6_ready"], 1)
                return [("t6_taken", upto(b, g, 1, 1))]

            def maximum(b, g, tiles):
                for n in tiles:
                    j, qt, kh = n // (2 * TT), n // 2 % TT, n % 2
                    if n == 0:
                        pe.wait_ge(qk_loaded[g], b * (16 * QK_DMAS) + 16 * QK_DMAS)
                    if not (isinstance(b, int) and upto(b, g, NS1, n) < 2):
                        pe.wait_ge(s["s1_taken"], upto(b, g, NS1, n - 1))
                    nc.tensor.matmul(ms[n % 2][:, :], qa[g][0:ROWS, j, qt * P:(qt + 1) * P],
                                     ka[g][0:ROWS, j, kh * 512:(kh + 1) * 512], start=True, stop=True
                                     ).then_inc(s["s1_ready"], 1)

            def transpose_maxima(b, g, bank_free):
                for what, n in bank_free:
                    wait_used(pe, s[what], n)
                pe.wait_ge(s["max_done"], upto(b, g, 1, 1))
                nc.tensor.transpose(job[0:HG * TT, 0:P], mx[:, :], id_sb[:, :]).then_inc(s["mx_ready"], 1)
                return [("mx_taken", upto(b, g, 1, 1))]

            def scores(b, g, st_, pair, first):
                qh, tt = st_ // TT, st_ % TT
                if st_ == 0 and pair == 0:
                    pe.wait_ge(s["m_loaded"], upto(b, g, 16, 16))
                if not (first and g == 0 and st_ == 0):
                    pe.wait_ge(s["exp_done"], upto(b, g, 2 * STEPS, 2 * st_ + pair - 1))
                for i in range(2):
                    j = 2 * pair + i
                    last = nc.tensor.matmul(sc[pair][:, i, :], ka[g][0:ROWS + MROWS, j, tt * P:(tt + 1) * P],
                                            qa[g][0:ROWS + MROWS, j, qh * NQ:(qh + 1) * NQ], start=True, stop=True)
                last.then_inc(s["s2_ready"], 1)

            def weigh(b, g, st_):
                qh, tt = st_ // TT, st_ % TT
                if st_ == 0:
                    pe.wait_ge(v_loaded[g % 2], b * 32 + (g // 2 + 1) * 16)
                    if isinstance(b, int) and b == 0 and g == 0:
                        pe.wait_ge(s["ob_zero"], 1)
                pe.wait_ge(s["exp_done"], upto(b, g, 2 * STEPS, 2 * st_ + 2))
                if tt == 0:
                    wait_used(pe, s["o_taken"], upto(b, g, QH, qh))
                for j in range(HG):
                    last = nc.tensor.matmul(ob[32 * j:32 * j + VW, :], v_sb[g % 2][:, tt, j, :], prob[st_ % 2][:, j, :],
                                            start=(tt == 0), stop=(tt == TT - 1))
                last.then_inc(s["pv_done"], 1)

            def batch(b, proj=True, tail=True, last=False, first=False):
                free = [("mx_taken", upto(b, 0, 1, 1))] + ([("t6_taken", upto(b, 0, 1, -G))] if tail else [])
                for g in range(G):
                    nxt = not (last and g == G - 1)
                    bn, gn = b + (g + 1) // G, (g + 1) % G
                    for st_ in range(STEPS):
                        tiles = list(maximum_tiles(st_)) if nxt else []
                        half = (len(tiles) + 1) // 2
                        scores(b, g, st_, 0, first)
                        maximum(bn, gn, tiles[:half])
                        scores(b, g, st_, 1, first)
                        for name, at in STEP_OF.items():
                            if at != st_:
                                continue
                            if name == "mx":
                                if nxt:
                                    free = transpose_maxima(bn, gn, free)
                            elif name in "eov":
                                if proj:
                                    free = proj_job(b + LEAD, g, name, free)
                            elif tail:
                                free = tail_job(b - 1, g, name, free)
                        maximum(bn, gn, tiles[half:])
                        if st_ > 0:
                            weigh(b, g, st_ - 1)
                        elif not (first and g == 0):
                            weigh(b + (g - 1) // G, (g - 1) % G, STEPS - 1)

            pe.wait_ge(s["consts_loaded"], 160)
            pe.wait_ge(s["ones_set"], 1)
            pe.wait_ge(s["abs_summed"], 2)
            nc.tensor.matmul(job[:, 0:2], ones[:, :], asum[:, :], start=True, stop=True).then_inc(s["sums_ready"], 1)
            pe.wait_ge(s["thresholds_set"], 1)
            for b in range(LEAD):
                free = [("v_taken", upto(b, 0, 1, 0))]
                for g in range(G):
                    for name in "eov":
                        free = proj_job(b, g, name, free)
            maximum(0, 0, range(NS1))
            transpose_maxima(0, 0, [("v_taken", LEAD * G)])
            pe.wait_ge(s["ternary_done"], 2)
            batch(0, tail=False, first=True)
            batch(1)
            with pe.Fori(2, B - LEAD) as b:
                batch(b)
            batch(B - 2, proj=False)
            batch(B - 1, proj=False, last=True)
            weigh(B - 1, G - 1, STEPS - 1)
            free = [("t6_taken", (B - 1) * G)]
            for g in range(G):
                for name in STEP_OF:
                    if name not in ("e", "o", "v", "mx"):
                        free = tail_job(B - 1, g, name, free)

        @block.scalar
        def _(act):
            def exps(b, g, st_, pair):
                act.wait_ge(s["s2_ready"], upto(b, g, 2 * STEPS, 2 * st_ + pair + 1))
                if pair == 0 and not (isinstance(b, int) and b == 0 and g == 0 and st_ < 2):
                    act.wait_ge(s["pv_done"], upto(b, g, STEPS, st_ - 1))
                nc.scalar.activation(prob[st_ % 2][:, 2 * pair:2 * pair + 2, :], sc[pair][:, :, :], ACT.Exp
                                     ).then_inc(s["exp_done"], 1)

            def take_outputs(b, g, qh):
                act.wait_ge(s["pv_done"], upto(b, g, STEPS, (qh + 1) * TT))
                wait_used(act, at_stored[qh], upto(b, g, 16, 0))
                nc.scalar.activation(at_st[qh][:, :], ob[:, :], ACT.Copy).then_inc(s["o_taken"], 1)

            def proj_job(b, g, name):
                eo = "eo".index(name)
                full = ("even", "odd")[eo]
                act.wait_ge(s[full + "_ready"], upto(b, g, 1, 1))
                wait_used(act, s["products"], upto(b, g, 4, 0))
                for i in range(2):
                    done = nc.scalar.activation((ev_sb, od_sb)[eo][:, i, :], job[:, i * TQ:(i + 1) * TQ], ACT.Identity,
                                                bias=bqk_sb[:, i, eo:eo + 1])
                done.then_inc(s[full + "_taken"], 1)

            def tail_job(b, g, name):
                if name in ("t2", "t4"):
                    act.wait_ge(s[name + "_ready"], upto(b, g, 1, 1))
                    dst = {"t2": att_t, "t4": h1_t}[name]
                    nc.scalar.activation(dst[:, :, :].rearrange("p c t -> p (c t)"), job[:, :], ACT.Copy
                                         ).then_inc(s[name + "_taken"], 1)
                if name[0] == "f":
                    n = int(name[1])
                    act.wait_ge(s["f_ready"], upto(b, g, FT // 2, n + 1))
                    for i in range(2):
                        f = 2 * n + i
                        nc.scalar.activation(hid[:, f, :], job[:, i * TQ:(i + 1) * TQ], ACT.Relu,
                                             bias=b1_sb[:, f:f + 1]).then_inc(s["f_taken"], 1)

            def batch(b, proj=True, tail=True, first=False):
                for g in range(G):
                    for st_ in range(STEPS):
                        exps(b, g, st_, 0)
                        if st_ == TT + 1:
                            take_outputs(b, g, 0)
                        if st_ == 1 and not (first and g == 0):
                            take_outputs(b + (g - 1) // G, (g - 1) % G, 1)
                        exps(b, g, st_, 1)
                        for name, at in STEP_OF.items():
                            if at == st_ and name in "eo" and proj:
                                proj_job(b + LEAD, g, name)
                            elif at == st_ and name not in "eo" and tail:
                                tail_job(b - 1, g, name)

            act.wait_ge(s["w1_loaded"], 16)
            nc.scalar.activation(prob[0][:, :, :].rearrange("p h q -> p (h q)"), w1_sb[:, :, :].rearrange("p c f -> p (c f)"),
                                 ACT.Abs, accum_out=asum[:, 0:1]).then_inc(s["abs_summed"], 1)
            act.wait_ge(s["w2_loaded"], 16)
            nc.scalar.activation(prob[1][:, :, :].rearrange("p h q -> p (h q)"), w2_sb[:, :, :].rearrange("p c f -> p (c f)"),
                                 ACT.Abs, accum_out=asum[:, 1:2]).then_inc(s["abs_summed"], 1)
            act.wait_ge(s["consts_loaded"], 160)
            act.wait_ge(s["abs_summed"], 2)
            for b in range(LEAD):
                for g in range(G):
                    for name in "eo":
                        proj_job(b, g, name)
            batch(0, tail=False, first=True)
            batch(1)
            with act.Fori(2, B - LEAD) as b:
                batch(b)
            batch(B - 2, proj=False)
            batch(B - 1, proj=False)
            take_outputs(B - 1, G - 1, 1)
            for g in range(G):
                for name in STEP_OF:
                    if name not in "eo":
                        tail_job(B - 1, g, name)

        @block.vector
        def _(dve):
            def maximum(b, g, tiles):
                for n in tiles:
                    if n == 0:
                        wait_used(dve, s["max_done"], upto(b, g, 1, 0))
                    dve.wait_ge(s["s1_ready"], upto(b, g, NS1, n + 1))
                    nc.vector.reduce_max(mxp[:, n % 2, n // 2:n // 2 + 1], ms[n % 2][:, :], AX.X
                                         ).then_inc(s["s1_taken"], 1)

            def combine(b, g):
                dve.wait_ge(s["s1_taken"], upto(b, g, NS1, NS1))
                wait_used(dve, s["mx_ready"], upto(b, g, 1, 0))
                nc.vector.tensor_tensor(mx[:, :], mxp[:, 0, :], mxp[:, 1, :], ALU.max).then_inc(s["max_done"], 1)

            def take_maxima(b, g):
                dve.wait_ge(s["mx_ready"], upto(b, g, 1, 1))
                wait_used(dve, s["m_stored"], upto(b, g, 16, 0))
                src = job[0:HG * TT, 0:P]
                nc.vector.tensor_scalar(nm[:, 0, :], src, -1.0, None, ALU.mult).then_inc(s["high_done"], 1)
                dve.wait_ge(s["high_done"], upto(b, g, 1, 1))
                nc.vector.scalar_tensor_tensor(out=nm[:, 1, :], in0=src, scalar=-1.0, in1=nm[:, 0, :],
                                               op0=ALU.mult, op1=ALU.subtract).then_inc(s["mx_taken"], 1)

            def take_v(b, g):
                dve.wait_ge(s["v_ready"], upto(b, g, 1, 1))
                wait_used(dve, s["v_stored"], upto(b, g, 16, 0))
                for tl in range(TL):
                    done = nc.vector.tensor_tensor(
                        v_st[:, :, tl, :, 0:HD], job[:, tl * D:(tl + 1) * D].rearrange("p (g h c) -> p g h c", g=G, h=HG),
                        bv_sb[:, :].rearrange("p (g h c) -> p g h c", g=G, h=HG), ALU.add)
                done.then_inc(s["v_taken"], 1)

            def moments_of(b, g, src_done, src, stats, moments, var, tag):
                dve.wait_ge(s[src_done], upto(b, g, 1, 1))
                nc.vector.bn_stats(stats[:, 0, :], src[:, 0, :]).then_inc(s["stats" + tag], 1)
                dve.wait_ge(s["stats" + tag], upto(b, g, TL, 1))
                nc.vector.bn_stats(stats[:, 1, :], src[:, 1, :]).then_inc(s["stats" + tag], 1)
                nc.vector.bn_aggr(moments[:, 0, :], stats[:, 0, :]).then_inc(s["moments" + tag], 1)
                dve.wait_ge(s["moments" + tag], upto(b, g, TL, 1))
                dve.wait_ge(s["stats" + tag], upto(b, g, TL, 2))
                nc.vector.tensor_scalar(var[:, 0:1], moments[:, 0, 1:2], EPS, None, ALU.add).then_inc(s["var" + tag], 1)
                nc.vector.bn_aggr(moments[:, 1, :], stats[:, 1, :]).then_inc(s["moments" + tag], 1)
                dve.wait_ge(s["moments" + tag], upto(b, g, TL, 2))
                nc.vector.tensor_scalar(var[:, 1:2], moments[:, 1, 1:2], EPS, None, ALU.add).then_inc(s["var" + tag], 1)

            def normalise(b, g, src, moments, power, dst, dst_done, tag):
                dve.wait_ge(s["rstd" + tag], upto(b, g, 1, 1))
                for tl in range(TL):
                    nc.vector.tensor_scalar(dst[:, tl, :], src[:, tl, :], moments[:, tl, 0:1], power[:, tl:tl + 1],
                                            ALU.subtract, ALU.mult).then_inc(s[dst_done], 1)

            def tail_job(b, g, name):
                if name in ("t1a", "t1b"):
                    tl = "ab".index(name[-1])
                    dve.wait_ge(s["t1_ready"], upto(b, g, TL, tl + 1))
                    heads = job[:, :].rearrange("p (h c) -> p h c", c=32)
                    nc.vector.reciprocal(rden[:, tl, :], heads[:, :, HD]).then_inc(s["recip_done"], 1)
                    dve.wait_ge(s["recip_done"], upto(b, g, TL, tl + 1))
                    nc.vector.tensor_tensor(att[:, tl, :].rearrange("p (h c) -> p h c", c=HD), heads[:, :, 0:HD],
                                            rden[:, tl, :].unsqueeze(2).broadcast_to([P, H, HD]), ALU.mult
                                            ).then_inc(s["t1_taken"], 1)
                elif name == "t3":
                    dve.wait_ge(s["t3_ready"], upto(b, g, 1, 1))
                    dve.wait_ge(s["xb_done"], upto(b, g, 1, 1))
                    nc.vector.tensor_tensor(y[:, :, :].rearrange("p t f -> p (t f)"), job[:, :],
                                            xb[:, :, :].rearrange("p t f -> p (t f)"), ALU.add
                                            ).then_inc(s["t3_taken"], 1)
                    moments_of(b, g, "t3_taken", y, st, mv, ve, "_done")
                elif name == "t6b":
                    dve.wait_ge(s["t6_ready"], upto(b, g, 1, 1))
                    dve.wait_ge(s["h1b_done"], upto(b, g, 1, 1))
                    nc.vector.tensor_tensor(y2[:, :, :].rearrange("p t f -> p (t f)"), job[:, :],
                                            h1b[:, :, :].rearrange("p t f -> p (t f)"), ALU.add
                                            ).then_inc(s["t6_taken"], 1)
                    moments_of(b, g, "t6_taken", y2, st2, mv2, ve2, "2_done")

            def finish_first_norm(b, g):
                normalise(b, g, y, mv, rstd, h1, "h1_done", "_done")

            def finish_second_norm(b, g):
                wait_used(dve, s["out_stored"], upto(b, g, 16, 0))
                normalise(b, g, y2, mv2, rstd2, res, "res_done", "2_done")

            def batch(b, proj=True, tail=True, last=False):
                for g in range(G):
                    nxt = not (last and g == G - 1)
                    bn, gn = b + (g + 1) // G, (g + 1) % G
                    for st_ in range(STEPS):
                        if nxt:
                            maximum(bn, gn, maximum_tiles(st_))
                        if st_ == MAX_STEPS - 1 and nxt:
                            combine(bn, gn)
                        if tail and st_ == STEP_OF["t3"] + 1:
                            finish_first_norm(b - 1, g)
                        for name, at in STEP_OF.items():
                            if at != st_:
                                continue
                            if name == "mx":
                                if nxt:
                                    take_maxima(bn, gn)
                            elif name == "v":
                                if proj:
                                    take_v(b + LEAD, g)
                            elif tail and name not in "eo":
                                tail_job(b - 1, g, name)
                    if tail:
                        finish_second_norm(b - 1, g)

            nc.vector.memset(ob[:, :], 0.0).then_inc(s["ob_zero"], 1)
            nc.vector.memset(v_st[:, :, :, :, :].rearrange("p g t h c -> p (g t h c)"), 1.0)
            for i in range(G):
                nc.vector.memset(ka[i][ROWS:ROWS + MROWS, :, :], 1.0)
            nc.vector.memset(ones[:, :], 1.0).then_inc(s["ones_set"], 1)
            dve.wait_ge(s["ones_set"], 1)
            dve.wait_ge(s["sums_ready"], 1)
            nc.vector.tensor_scalar(thr[:, 1, :], job[:, 0:2], 1.0 / (D * F), EPS, ALU.mult, ALU.add
                                    ).then_inc(s["thr_half"], 1)
            dve.wait_ge(s["thr_half"], 1)
            nc.vector.tensor_scalar(thr[:, 0, :], thr[:, 1, :], 0.5, None, ALU.mult).then_inc(s["thr_half"], 1)
            dve.wait_ge(s["thr_half"], 2)
            nc.vector.tensor_scalar(thr[:, 1, :], thr[:, 0, :], -1.0, None, ALU.mult).then_inc(s["thresholds_set"], 1)
            dve.wait_ge(s["thresholds_set"], 1)
            for i, w in enumerate((w1_sb, w2_sb)):
                flat = w[:, :, :].rearrange("p c f -> p (c f)")
                below = prob[i][:, :, :].rearrange("p h q -> p (h q)")
                nc.vector.tensor_scalar(below, flat, thr[:, 1, i:i + 1], None, ALU.is_lt).then_inc(s["signs_done"], 1)
                dve.wait_ge(s["signs_done"], i + 1)
                nc.vector.scalar_tensor_tensor(out=flat, in0=flat, scalar=thr[:, 0, i:i + 1], in1=below,
                                               op0=ALU.is_gt, op1=ALU.subtract).then_inc(s["ternary_done"], 1)
            dve.wait_ge(s["consts_loaded"], 160)
            for b in range(LEAD):
                for g in range(G):
                    take_v(b, g)
            maximum(0, 0, range(NS1))
            combine(0, 0)
            take_maxima(0, 0)
            batch(0, tail=False)
            batch(1)
            with dve.Fori(2, B - LEAD) as b:
                batch(b)
            batch(B - 2, proj=False)
            batch(B - 1, proj=False, last=True)
            for g in range(G):
                for name in STEP_OF:
                    if name == "t4":
                        finish_first_norm(B - 1, g)
                    if name not in ("e", "o", "v", "mx"):
                        tail_job(B - 1, g, name)
                finish_second_norm(B - 1, g)

        @block.gpsimd
        def _(pool):
            def tt(dst, a, b_, op):
                return nc.gpsimd.tensor_tensor(dst, a, b_, op)

            def proj(b, g):
                cos = cs_sb[:, 0, :, g * TQ:(g + 1) * TQ]
                sin = cs_sb[:, 1, :, g * TQ:(g + 1) * TQ]
                wait_used(pool, s["roped"], upto(b, g, 2, 0))
                pool.wait_ge(s["even_taken"], upto(b, g, 1, 1))
                tt(ec[:, :, :], ev_sb[:, :, :], cos, ALU.mult).then_inc(s["products"], 1)
                tt(es[:, :, :], ev_sb[:, :, :], sin, ALU.mult).then_inc(s["products"], 1)
                pool.wait_ge(s["odd_taken"], upto(b, g, 1, 1))
                tt(os_[:, :, :], od_sb[:, :, :], sin, ALU.mult).then_inc(s["products"], 1)
                tt(oc[:, :, :], od_sb[:, :, :], cos, ALU.mult).then_inc(s["products"], 1)
                pool.wait_ge(s["products"], upto(b, g, 4, 4))
                wait_used(pool, s["parts_stored"], upto(b, g, 32, 0))
                wait_used(pool, s["parts_done"], upto(b, g, 1, 0))
                tt(rot[:, :, 0, :], ec[:, :, :], os_[:, :, :], ALU.subtract)
                tt(rot[:, :, 1, :], es[:, :, :], oc[:, :, :], ALU.add)
                tt(parts[:, :, 0, 0, :], ec[:, :, :], os_[:, :, :], ALU.subtract).then_inc(s["roped"], 1)
                tt(parts[:, :, 1, 0, :], es[:, :, :], oc[:, :, :], ALU.add).then_inc(s["roped"], 1)
                pool.wait_ge(s["roped"], upto(b, g, 2, 2))
                tt(rest[:, :, :, :], rot[:, :, :, :], parts[:, :, :, 0, :], ALU.subtract).then_inc(s["rest_done"], 1)
                tt(parts[:, :, :, 1, :], rot[:, :, :, :], parts[:, :, :, 0, :], ALU.subtract).then_inc(s["mid_done"], 1)
                pool.wait_ge(s["rest_done"], upto(b, g, 1, 1))
                pool.wait_ge(s["mid_done"], upto(b, g, 1, 1))
                tt(parts[:, :, :, 2, :], rest[:, :, :, :], parts[:, :, :, 1, :], ALU.subtract).then_inc(s["parts_done"], 1)

            def add_bias(b, g, src_done, n, src, bias, dst, used, done):
                pool.wait_ge(s[src_done], n)
                wait_used(pool, s[used], upto(b, g, 1, 0))
                for tl in range(TL):
                    last = tt(dst[:, tl, :], src[:, tl, :], bias[:, :], ALU.add)
                last.then_inc(s[done], 1)

            def power(b, g, var, dst, tag):
                pool.wait_ge(s["var" + tag], upto(b, g, TL, TL))
                tt(dst[:, :], var[:, :], half_sb[:, :], ALU.pow).then_inc(s["rstd" + tag], 1)

            def tail(b, g):
                add_bias(b, g, "xn_loaded", upto(b, g, 16, 16), xn, bo_sb, xb, "t3_taken", "xb_done")
                power(b, g, ve, rstd, "_done")
                add_bias(b, g, "h1_done", upto(b, g, TL, TL), h1, b2_sb, h1b, "t6_taken", "h1b_done")
                power(b, g, ve2, rstd2, "2_done")

            nc.gpsimd.memset(half_sb[:, :], -0.5).then_inc(s["powers_set"], 1)
            pool.wait_ge(s["consts_loaded"], 160)
            pool.wait_ge(s["powers_set"], 1)
            for b in range(LEAD):
                for g in range(G):
                    proj(b, g)
            for g in range(G):
                proj(LEAD, g)
            for g in range(G):
                proj(1 + LEAD, g)
                tail(0, g)
            with pool.Fori(2, B - LEAD) as b:
                for g in range(G):
                    proj(b + LEAD, g)
                    tail(b - 1, g)
            for b in range(B - LEAD, B + 1):
                for g in range(G):
                    tail(b - 1, g)


def rope_table():
    one = np.float32(1.0)
    inv = one / np.float32(10000.0) ** (np.arange(0, HD, 2, dtype=np.float32) / np.float32(HD))
    angle = np.arange(S, dtype=np.float32)[None, :] * inv[:, None].astype(np.float32)
    table = np.stack([np.cos(angle), np.sin(angle)], axis=1)
    scale = np.array([HD ** -0.5, 1.0], np.float32)
    table = table[:, :, None, :] * scale[None, None, :, None]
    return np.ascontiguousarray(np.tile(table, (H, 1, 1, 1)).astype(np.float32))


def kernel(**inputs):
    import concourse.bacc as bacc
    from concourse.bass_utils import run_bass_kernel_spmd as run

    a = {n: np.asarray(v) for n, v in inputs.items()}

    def pairs(w):
        return np.moveaxis(w.reshape(H, HD // 2, 2, *w.shape[1:]), 2, 0).reshape(2, P, *w.shape[1:])

    wqk = np.stack([pairs(a["L0_attn_Wq"]), pairs(a["L0_attn_Wk"])])
    wqk = wqk.reshape(2, 2, P, KC, P).transpose(4, 3, 0, 1, 2)
    bqk = np.stack([pairs(a["L0_attn_bq"]), pairs(a["L0_attn_bk"])]).transpose(2, 0, 1)
    arrays = {
        "x": a["L0_attn_x"],
        "xt": a["L0_attn_x"].transpose(0, 2, 1),
        "wqk": wqk,
        "bqk": bqk,
        "wv": a["L0_attn_Wv"].T,
        "bv": a["L0_attn_bv"],
        "wo": a["L0_attn_Wo"].T,
        "bo": a["L0_attn_bo"],
        "w1": a["L0_ffn_W1"].T,
        "b1": a["L0_ffn_b1"].reshape(FT, P).T,
        "w2": a["L0_ffn_W2"].T,
        "b2": a["L0_ffn_b2"],
        "rope": rope_table(),
        "ident": np.eye(P, dtype=np.float32),
    }
    arrays = {n: np.ascontiguousarray(v) for n, v in arrays.items()}
    nc = bacc.Bacc("TRN2", target_bir_lowering=False, num_devices=1)
    args = [nc.dram_tensor(n, v.shape, mybir.dt.from_np(v.dtype), kind="ExternalInput").ap() for n, v in arrays.items()]
    args.append(nc.dram_tensor("out", (B, S, D), mybir.dt.float32, kind="ExternalOutput").ap())
    build(nc, *args)
    r = run(nc, [arrays], core_ids=[0])
    return r.results[0]["out"]
```

```python
import numpy as np

import concourse.bass as bass
from concourse import mybir
from contextlib import ExitStack

B, S, D = 16, 1024, 256
H, HD = 16, 16
F = 1024
P = 128
G = 4
HG = H // G
TQ = S // G
TL = TQ // P
TT = S // P
KC = D // P
FT = F // P
QH = 2
NQ = S // QH
STEPS = QH * TT
VW = HD + 1
PARTS = 3
TERMS = 6
ROWS = TERMS * HD
MROWS = 2
Q_PARTS = [0, 0, 1, 1, 0, 2]
K_PARTS = [0, 1, 0, 1, 2, 0]
EPS = 1e-5
NS1 = HG * TT * 2
MAX_AHEAD = 4

A_PIECES = {1: "e0 e1", 3: "o0 o1", 5: "v0 v1"}
B_PIECES = {8: "e0 e1", 10: "o0 o1", 14: "v0 v1"}
T_PIECES = {7: "t1a", 9: "t1b", 11: "t2", 12: "t3a", 13: "t3b", 17: "t4",
            19: "f0 f1", 21: "f2 f3", 23: "f4 f5", 25: "f6 f7",
            27: "g0 g1", 28: "g2 g3", 29: "g4 g5", 30: "g6 g7"}
NORM_SLOT = 16
MX_SLOT = 24
A_QUARTER = {0: 0, 1: 2, 2: 3}
B_QUARTER = {0: 1}


def pieces(g, slot, proj, tail, maxima):
    found = []
    if proj and g in A_QUARTER:
        found += [("proj", A_QUARTER[g], p) for p in A_PIECES.get(slot, "").split()]
    if proj and g in B_QUARTER:
        found += [("proj", B_QUARTER[g], p) for p in B_PIECES.get(slot, "").split()]
    if tail:
        found += [("tail", g, p) for p in T_PIECES.get(slot, "").split()]
    if maxima and slot == MX_SLOT:
        found.append(("mx", 0, "mx"))
    return found


def maximum_tiles(b, g, slot, part, last):
    n = 2 * slot + part
    per = NS1 // (4 * STEPS)
    ahead = 1 if n < 4 * (STEPS - MAX_AHEAD) else 2
    if last and g + ahead >= G:
        return b, g, range(0, 0)
    start = (n + 4 * MAX_AHEAD) % (4 * STEPS) * per
    return b + (g + ahead) // G, (g + ahead) % G, range(start, start + per)


def wait_used(engine, semaphore, count):
    if not isinstance(count, int) or count > 0:
        engine.wait_ge(semaphore, count)


def build(nc, x, xt, wqk, bqk, wv, bv, wo, bo, w1, b1, w2, b2, rope, ident, out):
    fp32 = mybir.dt.float32
    bf16 = mybir.dt.bfloat16
    fp32r = mybir.dt.float32r
    ALU = mybir.AluOpType
    ACT = mybir.ActivationFunctionType
    AX = mybir.AxisListType

    qk_d = nc.dram_tensor("qk_parts", (B, 2, D, PARTS, S), bf16).ap()
    v_d = nc.dram_tensor("v_ones", (B, G, P, TT * HG * VW), fp32).ap()
    at_d = nc.dram_tensor("attention", (B, G, P, S), fp32).ap()
    m_d = nc.dram_tensor("maxima", (B, G, MROWS, HG * S), bf16).ap()

    with ExitStack() as ctx:
        def sb(name, shape, dt=fp32):
            return ctx.enter_context(nc.sbuf_tensor(name, shape, dt))

        def pb(name, shape):
            return ctx.enter_context(nc.psum_tensor(name, shape, fp32))

        def sem(name):
            return ctx.enter_context(nc.semaphore(name))

        id_sb = sb("id_sb", [P, P])
        ones = sb("ones", [P, P])
        wqk_sb = sb("wqk_sb", [P, KC, 2, 2, P])
        bqk_sb = sb("bqk_sb", [P, 2, 2])
        wv_sb = sb("wv_sb", [P, KC, D])
        wo_sb = sb("wo_sb", [P, KC, D])
        w1_sb = sb("w1_sb", [P, KC, F], fp32r)
        w2_sb = sb("w2_sb", [P, FT, D], fp32r)
        b1_sb = sb("b1_sb", [P, FT])
        bv_sb = sb("bv_sb", [P, D])
        bo_sb = sb("bo_sb", [P, D])
        b2_sb = sb("b2_sb", [P, D])
        cs_sb = sb("cs_sb", [P, 2, 2, S])
        half_sb = sb("half_sb", [P, TL])
        asum = sb("asum", [P, 2])
        thr = sb("thr", [P, 2, 2])

        xt_sb = sb("xt_sb", [P, KC, TQ])
        ev_sb = sb("ev_sb", [P, 2, TQ])
        od_sb = sb("od_sb", [P, 2, TQ])
        ec = sb("ec", [P, 2, TQ])
        os_ = sb("os_", [P, 2, TQ])
        es = sb("es", [P, 2, TQ])
        oc = sb("oc", [P, 2, TQ])
        rot = sb("rot", [P, 2, 2, TQ])
        rest = sb("rest", [P, 2, 2, TQ])
        parts = sb("parts", [P, 2, 2, PARTS, TQ], bf16)
        v_st = sb("v_st", [P, G, TL, HG, VW])

        qa = [sb(f"qa{i}", [P, HG, S], bf16) for i in range(G)]
        ka = [sb(f"ka{i}", [P, HG, S], bf16) for i in range(G)]
        v_sb = [sb(f"v_sb{i}", [P, TT, HG, VW]) for i in range(2)]
        prob = [sb(f"prob{i}", [P, HG, NQ]) for i in range(2)]
        at_st = [sb(f"at_st{i}", [P, NQ]) for i in range(QH)]
        mxp = sb("mxp", [P, 2, HG * TT])
        mx = sb("mx", [P, HG * TT])
        nm = sb("nm", [HG * TT, MROWS, P], bf16)

        at_sb = sb("at_sb", [P, G, TQ])
        rden = sb("rden", [P, TL, H])
        att = sb("att", [P, TL, D])
        att_t = sb("att_t", [P, KC, TQ])
        xn = sb("xn", [P, TL, D])
        xb = sb("xb", [P, TL, D])
        y = sb("y", [P, TL, D])
        st = sb("st", [P, TL, 6])
        mv = sb("mv", [P, TL, 2])
        ve = sb("ve", [P, TL])
        rstd = sb("rstd", [P, TL])
        h1 = sb("h1", [P, TL, D])
        h1b = sb("h1b", [P, TL, D])
        h1_t = [sb(f"h1_t{i}", [P, KC * TQ], fp32r) for i in range(2)]
        hid = [sb(f"hid{i}", [P, TQ]) for i in range(2)]
        hid_r = [sb(f"hid_r{i}", [P, FT, TQ], fp32r) for i in range(2)]
        y2 = sb("y2", [P, TL, D])
        st2 = sb("st2", [P, TL, 6])
        mv2 = sb("mv2", [P, TL, 2])
        ve2 = sb("ve2", [P, TL])
        rstd2 = sb("rstd2", [P, TL])
        res = sb("res", [P, TL, D])

        sc = [pb(f"sc{i}", [P, 2, NQ]) for i in range(2)]
        ms = [pb(f"ms{i}", [P, 512]) for i in range(2)]
        ob = pb("ob", [P, NQ])
        job = pb("job", [P, 512])

        names = """weights_loaded rope_loaded consts_loaded w1_loaded w2_loaded abs_summed sums_ready thresholds_set thr_half signs_done ternary_done
            ones_set powers_set xt_loaded even_ready even_taken odd_ready odd_taken v_ready v_taken roped products
            rotated rest_done mid_done parts_done parts_stored v_stored
            m_stored m_loaded s1_ready s1_taken max_done mx_ready high_done mx_taken
            s2_ready exp_done pv_done o_taken ob_zero
            at_loaded t1_ready recip_done t1_taken t2_ready t2_taken t3_ready t3_taken y_done stats_done moments_done
            var_done rstd_done h1_done t4_ready t4_taken f_ready f_taken hid_high hid_low t4_high t6_ready t6_taken
            xn_loaded xb_done h1b_done y2_done stats2_done moments2_done var2_done rstd2_done res_done out_stored""".split()
        s = {n: sem(n) for n in names}
        qk_loaded = [sem(f"qk_loaded{i}") for i in range(G)]
        v_loaded = [sem(f"v_loaded{i}") for i in range(2)]
        at_stored = [sem(f"at_stored{i}") for i in range(QH)]

        def upto(b, g, each, n):
            return b * (G * each) + (g * each + n)

        block = ctx.enter_context(nc.Block())
        QK_DMAS = 2 * TERMS

        def rotate(wait, engine, b, g):
            tt = engine.tensor_tensor
            cos = cs_sb[:, 0, :, g * TQ:(g + 1) * TQ]
            sin = cs_sb[:, 1, :, g * TQ:(g + 1) * TQ]
            wait_used(wait, s["roped"], upto(b, g, 2, 0))
            wait.wait_ge(s["even_taken"], upto(b, g, 1, 1))
            tt(ec[:, :, :], ev_sb[:, :, :], cos, ALU.mult).then_inc(s["products"], 1)
            tt(es[:, :, :], ev_sb[:, :, :], sin, ALU.mult).then_inc(s["products"], 1)
            wait.wait_ge(s["odd_taken"], upto(b, g, 1, 1))
            tt(os_[:, :, :], od_sb[:, :, :], sin, ALU.mult).then_inc(s["products"], 1)
            tt(oc[:, :, :], od_sb[:, :, :], cos, ALU.mult).then_inc(s["products"], 1)
            wait.wait_ge(s["products"], upto(b, g, 4, 4))
            wait_used(wait, s["parts_stored"], upto(b, g, 32, 0))
            wait_used(wait, s["parts_done"], upto(b, g, 1, 0))
            tt(rot[:, :, 0, :], ec[:, :, :], os_[:, :, :], ALU.subtract)
            tt(rot[:, :, 1, :], es[:, :, :], oc[:, :, :], ALU.add)
            tt(parts[:, :, 0, 0, :], ec[:, :, :], os_[:, :, :], ALU.subtract).then_inc(s["roped"], 1)
            tt(parts[:, :, 1, 0, :], es[:, :, :], oc[:, :, :], ALU.add).then_inc(s["roped"], 1)

        def split(wait, engine, b, g):
            tt = engine.tensor_tensor
            wait.wait_ge(s["roped"], upto(b, g, 2, 2))
            tt(rest[:, :, :, :], rot[:, :, :, :], parts[:, :, :, 0, :], ALU.subtract).then_inc(s["rest_done"], 1)
            tt(parts[:, :, :, 1, :], rot[:, :, :, :], parts[:, :, :, 0, :], ALU.subtract).then_inc(s["mid_done"], 1)
            wait.wait_ge(s["rest_done"], upto(b, g, 1, 1))
            wait.wait_ge(s["mid_done"], upto(b, g, 1, 1))
            tt(parts[:, :, :, 2, :], rest[:, :, :, :], parts[:, :, :, 1, :], ALU.subtract).then_inc(s["parts_done"], 1)

        @block.sync
        def _(sp):
            def proj_in(b, g):
                wait_used(sp, s["v_ready"], upto(b, g, 1, 0))
                sp.dma_start(xt_sb[:, :, :], xt[b].rearrange("(c p) t -> p c t", p=P)[:, :, g * TQ:(g + 1) * TQ]
                             ).then_inc(s["xt_loaded"], 16)

            def proj_out(b, g):
                sp.wait_ge(s["v_taken"], upto(b, g, 1, 1))
                sp.dma_start(v_d[b].rearrange("g p n -> p g n")[:, :, g * TL * HG * VW:(g + 1) * TL * HG * VW],
                             v_st[:, :, :, :, :].rearrange("p g t h c -> p g (t h c)")).then_inc(s["v_stored"], 16)
                sp.wait_ge(s["parts_done"], upto(b, g, 1, 1))
                for i in range(2):
                    sp.dma_start(
                        qk_d[b, i].rearrange("(p e) a t -> p (e a) t", e=2)[:, :, g * TQ:(g + 1) * TQ],
                        parts[:, i].rearrange("p e a t -> p (e a) t")).then_inc(s["parts_stored"], 16)

            def load_qk(b, g):
                sp.wait_ge(s["parts_stored"], upto(b, G, 32, 0))
                for i, (dst, order) in enumerate(((qa[g], Q_PARTS), (ka[g], K_PARTS))):
                    rows = qk_d[b, i, g * HG * HD:(g + 1) * HG * HD].rearrange("(h r) a t -> a r h t", r=HD)
                    for n, a in enumerate(order):
                        sp.dma_start(dst[n * HD:(n + 1) * HD, :, :], rows[a]).then_inc(qk_loaded[g], 16)

            def load_v(b, g):
                sp.wait_ge(s["v_stored"], upto(b, G, 16, 0))
                sp.dma_start(v_sb[g % 2][:, :, :, :].rearrange("p t h c -> p (t h c)"), v_d[b, g]
                             ).then_inc(v_loaded[g % 2], 16)

            def move_maxima(b, g):
                sp.wait_ge(s["mx_taken"], upto(b, g, 1, 1))
                sp.dma_start(m_d[b, g].rearrange("m (r c) -> r m c", c=P), nm[:, :, :]).then_inc(s["m_stored"], 16)
                sp.wait_ge(s["m_stored"], upto(b, g, 16, 16))
                sp.dma_start(qa[g][ROWS:ROWS + MROWS, :, :].rearrange("p h t -> p (h t)"), m_d[b, g]
                             ).then_inc(s["m_loaded"], 16)

            def store_attention(b, g, qh):
                sp.wait_ge(s["o_taken"], upto(b, g, QH, qh + 1))
                sp.dma_start(at_d[b, g, :, qh * NQ:(qh + 1) * NQ], at_st[qh][:, :]).then_inc(at_stored[qh], 16)

            def tail_in(b, g):
                wait_used(sp, s["xb_done"], upto(b, g, 1, 0))
                if g == 0:
                    for qh in range(QH):
                        sp.wait_ge(at_stored[qh], upto(b, G, 16, 0))
                    wait_used(sp, s["t1_ready"], upto(b, g, TL, 0))
                sp.dma_start(xn[:, :, :], x[b, g * TQ:(g + 1) * TQ].rearrange("(t p) f -> p t f", p=P)
                             ).then_inc(s["xn_loaded"], 16)
                if g > 0:
                    wait_used(sp, s["t1_ready"], upto(b, g, TL, 0))
                sp.dma_start(at_sb[:, :, :], at_d[b].rearrange("g p t -> p g t")[:, :, g * TQ:(g + 1) * TQ]
                             ).then_inc(s["at_loaded"], 16)

            def tail_out(b, g):
                sp.wait_ge(s["res_done"], upto(b, g, TL, TL))
                sp.dma_start(out[b, g * TQ:(g + 1) * TQ].rearrange("(t p) f -> p t f", p=P), res[:, :, :]
                             ).then_inc(s["out_stored"], 16)

            def unit(b, g, proj, tail, last, first, tail_before):
                if proj and g in A_QUARTER:
                    proj_in(b + 1, A_QUARTER[g])
                if not (first and g == 0):
                    store_attention(b + (g - 1) // G, (g - 1) % G, 1)
                if not (last and g == G - 1):
                    load_v(b + (g + 1) // G, (g + 1) % G)
                if tail:
                    tail_in(b - 1, g)
                if tail if g else tail_before:
                    tail_out(b - 1 + (g - 1) // G, (g - 1) % G)
                if proj and g in B_QUARTER:
                    proj_in(b + 1, B_QUARTER[g])
                if proj and g in A_QUARTER:
                    proj_out(b + 1, A_QUARTER[g])
                if not (last and g >= 2):
                    load_qk(b + (g + 2) // G, (g + 2) % G)
                store_attention(b, g, 0)
                if proj and g in B_QUARTER:
                    proj_out(b + 1, B_QUARTER[g])
                if not (last and g == G - 1):
                    move_maxima(b + (g + 1) // G, (g + 1) % G)

            def batch(b, proj=True, tail=True, last=False, first=False, tail_before=True):
                for g in range(G):
                    unit(b, g, proj, tail, last, first, tail_before)

            proj_in(0, 0)
            sp.dma_start(wqk_sb[:, :, :, :, :], wqk).then_inc(s["weights_loaded"], 16)
            sp.dma_start(bqk_sb[:, :, :], bqk).then_inc(s["weights_loaded"], 16)
            sp.dma_start(wv_sb[:, :, :], wv.rearrange("(c p) f -> p c f", p=P)).then_inc(s["weights_loaded"], 16)
            sp.dma_start(bv_sb[:, :], bv.partition_broadcast(P)).then_inc(s["weights_loaded"], 16)
            sp.dma_start(cs_sb[:, :, :, :], rope).then_inc(s["rope_loaded"], 16)
            sp.dma_start(prob[0][:, :, :].rearrange("p h q -> p (h q)").rearrange("p (c f) -> p c f", c=KC),
                         w1.rearrange("(c p) f -> p c f", p=P)).then_inc(s["w1_loaded"], 16)
            sp.dma_start(prob[1][:, :, :].rearrange("p h q -> p (h q)").rearrange("p (c f) -> p c f", c=FT),
                         w2.rearrange("(c p) f -> p c f", p=P)).then_inc(s["w2_loaded"], 16)
            sp.dma_start(id_sb[:, :], ident).then_inc(s["consts_loaded"], 16)
            sp.dma_start(wo_sb[:, :, :], wo.rearrange("(c p) f -> p c f", p=P)).then_inc(s["consts_loaded"], 16)
            sp.dma_start(bo_sb[:, :], bo.partition_broadcast(P)).then_inc(s["consts_loaded"], 16)
            sp.dma_start(b2_sb[:, :], b2.partition_broadcast(P)).then_inc(s["consts_loaded"], 16)
            sp.dma_start(b1_sb[:, :], b1).then_inc(s["consts_loaded"], 16)
            for g in range(G):
                if g:
                    proj_in(0, g)
                proj_out(0, g)
            sp.wait_ge(s["abs_summed"], 2)
            load_qk(0, 0)
            load_qk(0, 1)
            load_v(0, 0)
            move_maxima(0, 0)
            batch(0, tail=False, first=True, tail_before=False)
            batch(1, tail_before=False)
            with sp.Fori(2, B - 1) as b:
                batch(b)
            batch(B - 1, proj=False, last=True)
            store_attention(B - 1, G - 1, 1)
            tail_out(B - 2, G - 1)
            for g in range(G):
                tail_in(B - 1, g)
                tail_out(B - 1, g)
            sp.wait_ge(s["out_stored"], 16 * B * G)

        @block.tensor
        def _(pe):
            def proj_piece(b, g, name, bank_free):
                kind, i = name[0], int(name[1])
                if name == "e0":
                    pe.wait_ge(s["xt_loaded"], upto(b, g, 16, 16))
                if i == 0:
                    for what, n in bank_free:
                        wait_used(pe, s[what], n)
                for c in range(KC):
                    if kind == "v":
                        last = nc.tensor.matmul(job[:, i * D:(i + 1) * D], xt_sb[:, c, i * P:(i + 1) * P],
                                                wv_sb[:, c, :], start=(c == 0), stop=(c == KC - 1))
                    else:
                        last = nc.tensor.matmul(job[:, i * TQ:(i + 1) * TQ], wqk_sb[:, c, i, "eo".index(kind), :],
                                                xt_sb[:, c, :], start=(c == 0), stop=(c == KC - 1))
                full = {"e": "even", "o": "odd", "v": "v"}[kind]
                if i == 1:
                    last.then_inc(s[full + "_ready"], 1)
                return [(full + "_taken", upto(b, g, 1, 1))]

            def tail_piece(b, g, name, bank_free):
                if name == "t1a":
                    pe.wait_ge(s["at_loaded"], upto(b, g, 16, 16))
                elif name == "t2":
                    pe.wait_ge(s["t1_taken"], upto(b, g, TL, TL))
                elif name == "t3a":
                    pe.wait_ge(s["t2_taken"], upto(b, g, 1, 1))
                elif name == "t4":
                    pe.wait_ge(s["h1_done"], upto(b, g, TL, TL))
                elif name == "f0":
                    pe.wait_ge(s["t4_taken"], upto(b, g, 1, 1))
                if name in ("t1a", "t1b", "t2", "t3a", "t4", "f0", "f2", "f4", "f6", "g0"):
                    for what, n in bank_free:
                        wait_used(pe, s[what], n)
                if name in ("t1a", "t1b"):
                    tl = "ab".index(name[-1])
                    for gg in range(G):
                        last = nc.tensor.transpose(job[:, gg * P:(gg + 1) * P], at_sb[:, gg, tl * P:(tl + 1) * P],
                                                   id_sb[:, :])
                    last.then_inc(s["t1_ready"], 1)
                    return [("t1_taken", upto(b, g, TL, tl + 1))]
                if name in ("t2", "t4"):
                    src = {"t2": att, "t4": h1}[name]
                    for c in range(KC):
                        for tl in range(TL):
                            last = nc.tensor.transpose(job[:, c * TQ + tl * P:c * TQ + (tl + 1) * P],
                                                       src[:, tl, c * P:(c + 1) * P], id_sb[:, :])
                    last.then_inc(s[name + "_ready"], 1)
                    return [(name + "_taken", upto(b, g, 1, 1))]
                if name in ("t3a", "t3b"):
                    tl = "ab".index(name[-1])
                    for c in range(KC):
                        last = nc.tensor.matmul(job[:, tl * D:(tl + 1) * D], att_t[:, c, tl * P:(tl + 1) * P],
                                                wo_sb[:, c, :], start=(c == 0), stop=(c == KC - 1))
                    if tl == TL - 1:
                        last.then_inc(s["t3_ready"], 1)
                    return [("t3_taken", upto(b, g, 1, 1))]
                n = int(name[1])
                if name[0] == "f":
                    for c in range(KC):
                        for part in range(2):
                            last = nc.tensor.matmul(
                                job[:, n % 2 * TQ:(n % 2 + 1) * TQ], w1_sb[:, c, n * P:(n + 1) * P],
                                h1_t[part][:, c * TQ:(c + 1) * TQ],
                                start=(c == 0 and part == 0), stop=(c == KC - 1 and part == 1))
                    if n % 2:
                        last.then_inc(s["f_ready"], 1)
                    return [("f_taken", upto(b, g, FT, n + 1))]
                tl = n // 4
                for f in range(2 * (n % 4), 2 * (n % 4) + 2):
                    if tl == 0:
                        pe.wait_ge(s["hid_low"], upto(b, g, FT, f + 1))
                    for part in range(2):
                        last = nc.tensor.matmul(job[:, tl * D:(tl + 1) * D], hid_r[part][:, f, tl * P:(tl + 1) * P],
                                                w2_sb[:, f, :], start=(f == 0 and part == 0),
                                                stop=(f == FT - 1 and part == 1))
                if n == 7:
                    last.then_inc(s["t6_ready"], 1)
                return [("t6_taken", upto(b, g, 1, 1))]

            def maximum(b, g, tiles):
                for n in tiles:
                    j, qt, kh = n // (2 * TT), n // 2 % TT, n % 2
                    if n == 0:
                        pe.wait_ge(qk_loaded[g], b * (16 * QK_DMAS) + 16 * QK_DMAS)
                    if not (isinstance(b, int) and upto(b, g, NS1, n) < 2):
                        pe.wait_ge(s["s1_taken"], upto(b, g, NS1, n - 1))
                    nc.tensor.matmul(ms[n % 2][:, :], qa[g][0:ROWS, j, qt * P:(qt + 1) * P],
                                     ka[g][0:ROWS, j, kh * 512:(kh + 1) * 512], start=True, stop=True
                                     ).then_inc(s["s1_ready"], 1)

            def transpose_maxima(b, g, bank_free):
                for what, n in bank_free:
                    wait_used(pe, s[what], n)
                pe.wait_ge(s["max_done"], upto(b, g, 1, 1))
                nc.tensor.transpose(job[0:HG * TT, 0:P], mx[:, :], id_sb[:, :]).then_inc(s["mx_ready"], 1)
                return [("mx_taken", upto(b, g, 1, 1))]

            def scores(b, g, st_, pair, first):
                qh, tt = st_ // TT, st_ % TT
                if st_ == 0 and pair == 0:
                    pe.wait_ge(s["m_loaded"], upto(b, g, 16, 16))
                if not (first and g == 0 and st_ == 0):
                    pe.wait_ge(s["exp_done"], upto(b, g, 2 * STEPS, 2 * st_ + pair - 1))
                for i in range(2):
                    j = 2 * pair + i
                    last = nc.tensor.matmul(sc[pair][:, i, :], ka[g][0:ROWS + MROWS, j, tt * P:(tt + 1) * P],
                                            qa[g][0:ROWS + MROWS, j, qh * NQ:(qh + 1) * NQ], start=True, stop=True)
                last.then_inc(s["s2_ready"], 1)

            def weigh(b, g, st_):
                qh, tt = st_ // TT, st_ % TT
                if st_ == 0:
                    pe.wait_ge(v_loaded[g % 2], b * 32 + (g // 2 + 1) * 16)
                    if isinstance(b, int) and b == 0 and g == 0:
                        pe.wait_ge(s["ob_zero"], 1)
                pe.wait_ge(s["exp_done"], upto(b, g, 2 * STEPS, 2 * st_ + 2))
                if tt == 0:
                    wait_used(pe, s["o_taken"], upto(b, g, QH, qh))
                for j in range(HG):
                    last = nc.tensor.matmul(ob[32 * j:32 * j + VW, :], v_sb[g % 2][:, tt, j, :], prob[st_ % 2][:, j, :],
                                            start=(tt == 0), stop=(tt == TT - 1))
                last.then_inc(s["pv_done"], 1)

            def batch(b, proj=True, tail=True, last=False, first=False):
                free = [("mx_taken", upto(b, 0, 1, 1))] + ([("t6_taken", upto(b, 0, 1, -G))] if tail else [])
                for g in range(G):
                    nxt = not (last and g == G - 1)
                    bn, gn = b + (g + 1) // G, (g + 1) % G
                    for st_ in range(STEPS):
                        for half in range(2):
                            scores(b, g, st_, half, first)
                            maximum(*maximum_tiles(b, g, 2 * st_ + half, 0, last))
                            for stage, q, name in pieces(g, 2 * st_ + half, proj, tail, nxt):
                                if stage == "mx":
                                    free = transpose_maxima(bn, gn, free)
                                elif stage == "proj":
                                    free = proj_piece(b + 1, q, name, free)
                                else:
                                    free = tail_piece(b - 1, q, name, free)
                            maximum(*maximum_tiles(b, g, 2 * st_ + half, 1, last))
                            if half and st_ > 0:
                                weigh(b, g, st_ - 1)
                            elif half and not (first and g == 0):
                                weigh(b + (g - 1) // G, (g - 1) % G, STEPS - 1)

            pe.wait_ge(s["ones_set"], 1)
            pe.wait_ge(s["weights_loaded"], 64)
            free = []
            for g in range(G):
                for name in ("e0", "e1", "o0", "o1", "v0", "v1"):
                    free = proj_piece(0, g, name, free)
            pe.wait_ge(s["v_taken"], G)
            pe.wait_ge(s["abs_summed"], 2)
            nc.tensor.matmul(job[:, 0:2], ones[:, :], asum[:, :], start=True, stop=True).then_inc(s["sums_ready"], 1)
            maximum(0, 0, range(NS1))
            pe.wait_ge(s["consts_loaded"], 80)
            pe.wait_ge(s["thr_half"], 1)
            transpose_maxima(0, 0, [])
            maximum(0, 1, range(NS1 * MAX_AHEAD // STEPS))
            pe.wait_ge(s["ternary_done"], 2)
            batch(0, tail=False, first=True)
            batch(1)
            with pe.Fori(2, B - 1) as b:
                batch(b)
            batch(B - 1, proj=False, last=True)
            weigh(B - 1, G - 1, STEPS - 1)
            free = [("t6_taken", (B - 1) * G)]
            for g in range(G):
                for slot in range(2 * STEPS):
                    for stage, q, name in pieces(g, slot, False, True, False):
                        free = tail_piece(B - 1, g, name, free)

        @block.scalar
        def _(act):
            def exps(b, g, st_, pair):
                act.wait_ge(s["s2_ready"], upto(b, g, 2 * STEPS, 2 * st_ + pair + 1))
                if pair == 0 and not (isinstance(b, int) and b == 0 and g == 0 and st_ < 2):
                    act.wait_ge(s["pv_done"], upto(b, g, STEPS, st_ - 1))
                nc.scalar.activation(prob[st_ % 2][:, 2 * pair:2 * pair + 2, :], sc[pair][:, :, :], ACT.Exp
                                     ).then_inc(s["exp_done"], 1)

            def take_outputs(b, g, qh):
                act.wait_ge(s["pv_done"], upto(b, g, STEPS, (qh + 1) * TT))
                wait_used(act, at_stored[qh], upto(b, g, 16, 0))
                nc.scalar.activation(at_st[qh][:, :], ob[:, :], ACT.Copy).then_inc(s["o_taken"], 1)

            def proj_piece(b, g, name):
                if name not in ("e1", "o1"):
                    return
                eo = "eo".index(name[0])
                full = ("even", "odd")[eo]
                act.wait_ge(s[full + "_ready"], upto(b, g, 1, 1))
                wait_used(act, s["products"], upto(b, g, 4, 0))
                for i in range(2):
                    done = nc.scalar.activation((ev_sb, od_sb)[eo][:, i, :], job[:, i * TQ:(i + 1) * TQ], ACT.Identity,
                                                bias=bqk_sb[:, i, eo:eo + 1])
                done.then_inc(s[full + "_taken"], 1)

            def tail_piece(b, g, name):
                if name == "t2":
                    act.wait_ge(s["t2_ready"], upto(b, g, 1, 1))
                    nc.scalar.activation(att_t[:, :, :].rearrange("p c t -> p (c t)"), job[:, :], ACT.Copy
                                         ).then_inc(s["t2_taken"], 1)
                if name == "t4":
                    act.wait_ge(s["t4_ready"], upto(b, g, 1, 1))
                    nc.scalar.activation(h1_t[0][:, :], job[:, :], ACT.Copy).then_inc(s["t4_high"], 1)
                if name in ("f1", "f3", "f5", "f7"):
                    n = int(name[1])
                    act.wait_ge(s["f_ready"], upto(b, g, FT // 2, n // 2 + 1))
                    for i in range(2):
                        f = n - 1 + i
                        src, bias = job[:, i * TQ:(i + 1) * TQ], b1_sb[:, f:f + 1]
                        nc.scalar.activation(hid_r[0][:, f, :], src, ACT.Relu, bias=bias).then_inc(s["hid_high"], 1)
                        wait_used(act, s["hid_low"], upto(b, g, FT, f - 1))
                        nc.scalar.activation(hid[i][:, :], src, ACT.Relu, bias=bias).then_inc(s["f_taken"], 1)

            def batch(b, proj=True, tail=True, first=False):
                for g in range(G):
                    for st_ in range(STEPS):
                        for half in range(2):
                            exps(b, g, st_, half)
                            if st_ == TT + 1 and half == 0:
                                take_outputs(b, g, 0)
                            if st_ == 1 and half == 0 and not (first and g == 0):
                                take_outputs(b + (g - 1) // G, (g - 1) % G, 1)
                            for stage, q, name in pieces(g, 2 * st_ + half, proj, tail, False):
                                if stage == "proj":
                                    proj_piece(b + 1, q, name)
                                else:
                                    tail_piece(b - 1, q, name)

            act.wait_ge(s["weights_loaded"], 64)
            for g in range(G):
                for name in ("e1", "o1"):
                    proj_piece(0, g, name)
                if g < 2:
                    act.wait_ge(s[("w1_loaded", "w2_loaded")[g]], 16)
                    nc.scalar.activation(qa[g][:, 0:2, :].rearrange("p h q -> p (h q)"),
                                         prob[g][:, :, :].rearrange("p h q -> p (h q)"),
                                         ACT.Abs, accum_out=asum[:, g:g + 1]).then_inc(s["abs_summed"], 1)
            act.wait_ge(s["consts_loaded"], 80)
            act.wait_ge(s["ternary_done"], 2)
            batch(0, tail=False, first=True)
            batch(1)
            with act.Fori(2, B - 1) as b:
                batch(b)
            batch(B - 1, proj=False)
            take_outputs(B - 1, G - 1, 1)
            for g in range(G):
                for slot in range(2 * STEPS):
                    for stage, q, name in pieces(g, slot, False, True, False):
                        tail_piece(B - 1, g, name)

        @block.vector
        def _(dve):
            def maximum(b, g, tiles):
                for n in tiles:
                    if n == 0:
                        wait_used(dve, s["max_done"], upto(b, g, 1, 0))
                    dve.wait_ge(s["s1_ready"], upto(b, g, NS1, n + 1))
                    nc.vector.reduce_max(mxp[:, n % 2, n // 2:n // 2 + 1], ms[n % 2][:, :], AX.X
                                         ).then_inc(s["s1_taken"], 1)

            def combine(b, g):
                dve.wait_ge(s["s1_taken"], upto(b, g, NS1, NS1))
                wait_used(dve, s["mx_ready"], upto(b, g, 1, 0))
                nc.vector.tensor_tensor(mx[:, :], mxp[:, 0, :], mxp[:, 1, :], ALU.max).then_inc(s["max_done"], 1)

            def take_maxima(b, g):
                dve.wait_ge(s["mx_ready"], upto(b, g, 1, 1))
                wait_used(dve, s["m_stored"], upto(b, g, 16, 0))
                src = job[0:HG * TT, 0:P]
                nc.vector.tensor_scalar(nm[:, 0, :], src, -1.0, None, ALU.mult).then_inc(s["high_done"], 1)
                dve.wait_ge(s["high_done"], upto(b, g, 1, 1))
                nc.vector.scalar_tensor_tensor(out=nm[:, 1, :], in0=src, scalar=-1.0, in1=nm[:, 0, :],
                                               op0=ALU.mult, op1=ALU.subtract).then_inc(s["mx_taken"], 1)

            def take_v(b, g):
                dve.wait_ge(s["v_ready"], upto(b, g, 1, 1))
                wait_used(dve, s["v_stored"], upto(b, g, 16, 0))
                for tl in range(TL):
                    done = nc.vector.tensor_tensor(
                        v_st[:, :, tl, :, 0:HD], job[:, tl * D:(tl + 1) * D].rearrange("p (g h c) -> p g h c", g=G, h=HG),
                        bv_sb[:, :].rearrange("p (g h c) -> p g h c", g=G, h=HG), ALU.add)
                done.then_inc(s["v_taken"], 1)

            def moments_of(b, g, src_done, src, stats, moments, var, tag):
                dve.wait_ge(s[src_done], upto(b, g, 1, 1))
                nc.vector.bn_stats(stats[:, 0, :], src[:, 0, :]).then_inc(s["stats" + tag], 1)
                dve.wait_ge(s["stats" + tag], upto(b, g, TL, 1))
                nc.vector.bn_stats(stats[:, 1, :], src[:, 1, :]).then_inc(s["stats" + tag], 1)
                nc.vector.bn_aggr(moments[:, 0, :], stats[:, 0, :]).then_inc(s["moments" + tag], 1)
                dve.wait_ge(s["moments" + tag], upto(b, g, TL, 1))
                dve.wait_ge(s["stats" + tag], upto(b, g, TL, 2))
                nc.vector.tensor_scalar(var[:, 0:1], moments[:, 0, 1:2], EPS, None, ALU.add).then_inc(s["var" + tag], 1)
                nc.vector.bn_aggr(moments[:, 1, :], stats[:, 1, :]).then_inc(s["moments" + tag], 1)
                dve.wait_ge(s["moments" + tag], upto(b, g, TL, 2))
                nc.vector.tensor_scalar(var[:, 1:2], moments[:, 1, 1:2], EPS, None, ALU.add).then_inc(s["var" + tag], 1)

            def normalise(b, g, src, moments, power, dst, dst_done, tag):
                dve.wait_ge(s["rstd" + tag], upto(b, g, 1, 1))
                for tl in range(TL):
                    nc.vector.tensor_scalar(dst[:, tl, :], src[:, tl, :], moments[:, tl, 0:1], power[:, tl:tl + 1],
                                            ALU.subtract, ALU.mult).then_inc(s[dst_done], 1)

            def tail_piece(b, g, name):
                if name in ("t1a", "t1b"):
                    tl = "ab".index(name[-1])
                    dve.wait_ge(s["t1_ready"], upto(b, g, TL, tl + 1))
                    heads = job[:, :].rearrange("p (h c) -> p h c", c=32)
                    nc.vector.reciprocal(rden[:, tl, :], heads[:, :, HD]).then_inc(s["recip_done"], 1)
                    dve.wait_ge(s["recip_done"], upto(b, g, TL, tl + 1))
                    nc.vector.tensor_tensor(att[:, tl, :].rearrange("p (h c) -> p h c", c=HD), heads[:, :, 0:HD],
                                            rden[:, tl, :].unsqueeze(2).broadcast_to([P, H, HD]), ALU.mult
                                            ).then_inc(s["t1_taken"], 1)
                elif name == "t4":
                    dve.wait_ge(s["t4_high"], upto(b, g, 1, 1))
                    nc.vector.tensor_tensor(h1_t[1][:, :], job[:, :], h1_t[0][:, :], ALU.subtract
                                            ).then_inc(s["t4_taken"], 1)
                elif name == "t3b":
                    dve.wait_ge(s["t3_ready"], upto(b, g, 1, 1))
                    dve.wait_ge(s["xb_done"], upto(b, g, 1, 1))
                    nc.vector.tensor_tensor(y[:, :, :].rearrange("p t f -> p (t f)"), job[:, :],
                                            xb[:, :, :].rearrange("p t f -> p (t f)"), ALU.add
                                            ).then_inc(s["t3_taken"], 1)
                    moments_of(b, g, "t3_taken", y, st, mv, ve, "_done")
                elif name == "g7":
                    dve.wait_ge(s["t6_ready"], upto(b, g, 1, 1))
                    dve.wait_ge(s["h1b_done"], upto(b, g, 1, 1))
                    nc.vector.tensor_tensor(y2[:, :, :].rearrange("p t f -> p (t f)"), job[:, :],
                                            h1b[:, :, :].rearrange("p t f -> p (t f)"), ALU.add
                                            ).then_inc(s["t6_taken"], 1)
                    moments_of(b, g, "t6_taken", y2, st2, mv2, ve2, "2_done")

            def finish_first_norm(b, g):
                normalise(b, g, y, mv, rstd, h1, "h1_done", "_done")

            def finish_second_norm(b, g):
                wait_used(dve, s["out_stored"], upto(b, g, 16, 0))
                normalise(b, g, y2, mv2, rstd2, res, "res_done", "2_done")

            def batch(b, proj=True, tail=True, last=False, tail_before=True):
                for g in range(G):
                    nxt = not (last and g == G - 1)
                    bn, gn = b + (g + 1) // G, (g + 1) % G
                    for slot in range(2 * STEPS):
                        for part in range(2):
                            maximum(*maximum_tiles(b, g, slot, part, last))
                        if nxt and slot == 2 * (STEPS - MAX_AHEAD) - 1:
                            combine(bn, gn)
                        if slot == 1 and (tail if g else tail_before):
                            finish_second_norm(b - 1 + (g - 1) // G, (g - 1) % G)
                        if tail and slot == NORM_SLOT:
                            finish_first_norm(b - 1, g)
                        for stage, q, name in pieces(g, slot, proj, tail, nxt):
                            if stage == "mx":
                                take_maxima(bn, gn)
                            elif name == "v1":
                                take_v(b + 1, q)
                            elif stage == "tail":
                                tail_piece(b - 1, q, name)

            nc.vector.memset(ob[:, :], 0.0).then_inc(s["ob_zero"], 1)
            nc.vector.memset(v_st[:, :, :, :, :].rearrange("p g t h c -> p (g t h c)"), 1.0)
            for i in range(G):
                nc.vector.memset(ka[i][ROWS:ROWS + MROWS, :, :], 1.0)
            nc.vector.memset(ones[:, :], 1.0).then_inc(s["ones_set"], 1)
            dve.wait_ge(s["ones_set"], 1)
            dve.wait_ge(s["weights_loaded"], 64)
            dve.wait_ge(s["rope_loaded"], 16)
            for g in range(G):
                rotate(dve, nc.vector, 0, g)
                split(dve, nc.vector, 0, g)
                take_v(0, g)
            dve.wait_ge(s["sums_ready"], 1)
            nc.vector.tensor_scalar(thr[:, 1, :], job[:, 0:2], 1.0 / (D * F), EPS, ALU.mult, ALU.add
                                    ).then_inc(s["thr_half"], 1)
            dve.wait_ge(s["thr_half"], 1)
            nc.vector.tensor_scalar(thr[:, 0, :], thr[:, 1, :], 0.5, None, ALU.mult).then_inc(s["thr_half"], 1)
            dve.wait_ge(s["thr_half"], 2)
            nc.vector.tensor_scalar(thr[:, 1, :], thr[:, 0, :], -1.0, None, ALU.mult).then_inc(s["thresholds_set"], 1)
            dve.wait_ge(s["thresholds_set"], 1)
            for i, w in enumerate((w1_sb, w2_sb)):
                raw = prob[i][:, :, :].rearrange("p h q -> p (h q)")
                below = qa[2][:, 0:2, :].rearrange("p h q -> p (h q)")
                if i:
                    dve.wait_ge(s["ternary_done"], i)
                nc.vector.tensor_scalar(below, raw, thr[:, 1, i:i + 1], None, ALU.is_lt).then_inc(s["signs_done"], 1)
                dve.wait_ge(s["signs_done"], i + 1)
                nc.vector.scalar_tensor_tensor(out=w[:, :, :].rearrange("p c f -> p (c f)"), in0=raw, scalar=thr[:, 0, i:i + 1], in1=below,
                                               op0=ALU.is_gt, op1=ALU.subtract).then_inc(s["ternary_done"], 1)
            maximum(0, 0, range(NS1))
            combine(0, 0)
            take_maxima(0, 0)
            maximum(0, 1, range(NS1 * MAX_AHEAD // STEPS))
            batch(0, tail=False, tail_before=False)
            batch(1, tail_before=False)
            with dve.Fori(2, B - 1) as b:
                batch(b)
            batch(B - 1, proj=False, last=True)
            finish_second_norm(B - 2, G - 1)
            for g in range(G):
                for slot in range(2 * STEPS):
                    if slot == NORM_SLOT:
                        finish_first_norm(B - 1, g)
                    for stage, q, name in pieces(g, slot, False, True, False):
                        tail_piece(B - 1, g, name)
                finish_second_norm(B - 1, g)

        @block.gpsimd
        def _(pool):
            def add_bias(b, g, src_done, n, src, bias, dst, used, done):
                pool.wait_ge(s[src_done], n)
                wait_used(pool, s[used], upto(b, g, 1, 0))
                for tl in range(TL):
                    last = nc.gpsimd.tensor_tensor(dst[:, tl, :], src[:, tl, :], bias[:, :], ALU.add)
                last.then_inc(s[done], 1)

            def power(b, g, var, dst, tag):
                pool.wait_ge(s["var" + tag], upto(b, g, TL, TL))
                nc.gpsimd.tensor_tensor(dst[:, :], var[:, :], half_sb[:, :], ALU.pow).then_inc(s["rstd" + tag], 1)

            def low_parts(b, g, tiles):
                for f in tiles:
                    pool.wait_ge(s["f_taken"], upto(b, g, FT, f + 1))
                    pool.wait_ge(s["hid_high"], upto(b, g, FT, f + 1))
                    nc.gpsimd.tensor_tensor(hid_r[1][:, f, :], hid[f % 2][:, :], hid_r[0][:, f, :], ALU.subtract
                                            ).then_inc(s["hid_low"], 1)

            def unit(b, g, proj, tail):
                if proj and g in A_QUARTER:
                    rotate(pool, nc.gpsimd, b + 1, A_QUARTER[g])
                    split(pool, nc.gpsimd, b + 1, A_QUARTER[g])
                if tail:
                    add_bias(b - 1, g, "xn_loaded", upto(b - 1, g, 16, 16), xn, bo_sb, xb, "t3_taken", "xb_done")
                    power(b - 1, g, ve, rstd, "_done")
                if proj and g in B_QUARTER:
                    rotate(pool, nc.gpsimd, b + 1, B_QUARTER[g])
                if tail:
                    add_bias(b - 1, g, "h1_done", upto(b - 1, g, TL, TL), h1, b2_sb, h1b, "t6_taken", "h1b_done")
                    low_parts(b - 1, g, range(FT // 2))
                if proj and g in B_QUARTER:
                    split(pool, nc.gpsimd, b + 1, B_QUARTER[g])
                if tail:
                    low_parts(b - 1, g, range(FT // 2, FT))
                    power(b - 1, g, ve2, rstd2, "2_done")

            nc.gpsimd.memset(half_sb[:, :], -0.5).then_inc(s["powers_set"], 1)
            pool.wait_ge(s["consts_loaded"], 80)
            pool.wait_ge(s["rope_loaded"], 16)
            pool.wait_ge(s["powers_set"], 1)
            for b in (0, 1):
                for g in range(G):
                    unit(b, g, True, b > 0)
            with pool.Fori(2, B - 1) as b:
                for g in range(G):
                    unit(b, g, True, True)
            for b in (B - 1, B):
                for g in range(G):
                    unit(b, g, False, True)


def rope_table():
    one = np.float32(1.0)
    inv = one / np.float32(10000.0) ** (np.arange(0, HD, 2, dtype=np.float32) / np.float32(HD))
    angle = np.arange(S, dtype=np.float32)[None, :] * inv[:, None].astype(np.float32)
    table = np.stack([np.cos(angle), np.sin(angle)], axis=1)
    scale = np.array([HD ** -0.5, 1.0], np.float32)
    table = table[:, :, None, :] * scale[None, None, :, None]
    return np.ascontiguousarray(np.tile(table, (H, 1, 1, 1)).astype(np.float32))


def kernel(**inputs):
    import concourse.bacc as bacc
    from concourse.bass_utils import run_bass_kernel_spmd as run

    a = {n: np.asarray(v) for n, v in inputs.items()}

    def pairs(w):
        return np.moveaxis(w.reshape(H, HD // 2, 2, *w.shape[1:]), 2, 0).reshape(2, P, *w.shape[1:])

    wqk = np.stack([pairs(a["L0_attn_Wq"]), pairs(a["L0_attn_Wk"])])
    wqk = wqk.reshape(2, 2, P, KC, P).transpose(4, 3, 0, 1, 2)
    bqk = np.stack([pairs(a["L0_attn_bq"]), pairs(a["L0_attn_bk"])]).transpose(2, 0, 1)
    arrays = {
        "x": a["L0_attn_x"],
        "xt": a["L0_attn_x"].transpose(0, 2, 1),
        "wqk": wqk,
        "bqk": bqk,
        "wv": a["L0_attn_Wv"].T,
        "bv": a["L0_attn_bv"],
        "wo": a["L0_attn_Wo"].T,
        "bo": a["L0_attn_bo"],
        "w1": a["L0_ffn_W1"].T,
        "b1": a["L0_ffn_b1"].reshape(FT, P).T,
        "w2": a["L0_ffn_W2"].T,
        "b2": a["L0_ffn_b2"],
        "rope": rope_table(),
        "ident": np.eye(P, dtype=np.float32),
    }
    arrays = {n: np.ascontiguousarray(v) for n, v in arrays.items()}
    nc = bacc.Bacc("TRN2", target_bir_lowering=False, num_devices=1)
    args = [nc.dram_tensor(n, v.shape, mybir.dt.from_np(v.dtype), kind="ExternalInput").ap() for n, v in arrays.items()]
    args.append(nc.dram_tensor("out", (B, S, D), mybir.dt.float32, kind="ExternalOutput").ap())
    build(nc, *args)
    r = run(nc, [arrays], core_ids=[0])
    return r.results[0]["out"]
```

```python
import numpy as np

import concourse.bass as bass
from concourse import mybir
from contextlib import ExitStack

B, S, D = 16, 1024, 256
H, HD = 16, 16
F = 1024
P = 128
G = 4
HG = H // G
TQ = S // G
TL = TQ // P
TT = S // P
KC = D // P
FT = F // P
QH = 2
NQ = S // QH
STEPS = QH * TT
VW = HD + 1
PARTS = 3
TERMS = 6
ROWS = TERMS * HD
MROWS = 2
Q_PARTS = [0, 0, 1, 1, 0, 2]
K_PARTS = [0, 1, 0, 1, 2, 0]
EPS = 1e-5
NS1 = HG * TT * 2
MAX_AHEAD = 8

PROJ_PIECES = {1: [{2: "e0 e1", 4: "o0 o1", 15: "v0 v1"}],
               2: [{1: "e0 e1", 3: "o0 o1", 5: "v0 v1"},
                   {9: "e0 e1", 11: "o0 o1", 13: "v0 v1"}]}
T_PIECES = {6: "t1a", 8: "t1b", 10: "t2", 12: "t3a t3b", 18: "t4",
            20: "f0 f1", 22: "f2 f3", 24: "f4 f5", 26: "f6 f7",
            28: "g0 g1", 29: "g2 g3", 30: "g4 g5", 31: "g6 g7"}
SPLIT_SLOT = 28
SECOND_SPLIT_SLOT = 6
MX_SLOT = 16
FIRST_NORM = {(12, 1): "sum 0", (13, 0): "sum 1", (13, 1): "stats 0", (14, 0): "stats 1", (14, 1): "moments 0",
              (16, 1): "norm 0", (17, 0): "norm 1"}
SECOND_NORM = {(0, 0): "sum 0", (0, 1): "sum 1", (1, 0): "stats 0", (1, 1): "stats 1", (2, 0): "moments 0"}
LOW_MAXIMA_AT = (17, 1)


def projected(b, g):
    if isinstance(b, int) and b == 0 and g < 2:
        return [(1, 2 * g), (1, 2 * g + 1)]
    batch, quarter = (b + 1, g + 2) if g < 2 else (b + 2, g - 2)
    return [] if isinstance(batch, int) and batch >= B else [(batch, quarter)]


def projected_next(b, g):
    return projected(b + (g + 1) // G, (g + 1) % G)[:1]


def pieces(b, g, slot, tail, maxima):
    found = []
    proj = projected(b, g)
    for at, table in zip(proj, PROJ_PIECES.get(len(proj), [])):
        found += [("proj", at, p) for p in table.get(slot, "").split()]
    if tail:
        found += [("tail", (b - 1, g), p) for p in T_PIECES.get(slot, "").split()]
    if maxima and slot == MX_SLOT:
        found.append(("mx", (b + (g + 1) // G, (g + 1) % G), "mx"))
    return found


def maximum_tiles(b, g, n, last):
    per = NS1 // (4 * STEPS)
    before = 4 * (STEPS - MAX_AHEAD)
    if isinstance(b, int) and b == g == 0 and n < before:
        return 0, 1, range(n * NS1 // before, (n + 1) * NS1 // before)
    ahead = 1 if n < before else 2
    if last and g + ahead >= G:
        return b, g, range(0, 0)
    start = (n + 4 * MAX_AHEAD) % (4 * STEPS) * per
    return b + (g + ahead) // G, (g + ahead) % G, range(start, start + per)


END_STEPS = """new t1a, old f0, old f1, new t1b, old f2, old f3, new t2, old f4, old f5, new t3a, new t3b, old f6, old f7,
               new sum 0, new sum 1, old g0, old g1, new stats 0, new stats 1, old g2, old g3, new moments 0,
               old g4, old g5, old g6, old g7, new norm 0, new norm 1, after sum 0, after sum 1, new t4,
               after stats 0, after stats 1, after moments 0""".replace("\n", " ")


def end_steps():
    for quarter in range(G + 1):
        for step in END_STEPS.split(", "):
            kind, name = step.strip().split(" ", 1)
            at = quarter if kind == "new" else quarter - 1
            if 0 <= at < G:
                yield kind, at, name


def wait_used(engine, semaphore, count):
    if not isinstance(count, int) or count > 0:
        engine.wait_ge(semaphore, count)


def build(nc, x, xt, wqk, bqk, wv, bvc, wo, bo, w1, b1, w2, b2, rope, ident, out):
    fp32 = mybir.dt.float32
    bf16 = mybir.dt.bfloat16
    fp32r = mybir.dt.float32r
    ALU = mybir.AluOpType
    ACT = mybir.ActivationFunctionType
    AX = mybir.AxisListType

    qk_d = nc.dram_tensor("qk_parts", (B, 2, D, PARTS, S), bf16).ap()
    v_d = nc.dram_tensor("v_ones", (B, G, P, TT * HG * VW), fp32).ap()
    at_d = nc.dram_tensor("attention", (B, G, P, S), fp32).ap()
    m_d = nc.dram_tensor("maxima", (B, G, MROWS, HG * S), bf16).ap()

    with ExitStack() as ctx:
        def sb(name, shape, dt=fp32):
            return ctx.enter_context(nc.sbuf_tensor(name, shape, dt))

        def pb(name, shape):
            return ctx.enter_context(nc.psum_tensor(name, shape, fp32))

        def sem(name):
            return ctx.enter_context(nc.semaphore(name))

        id_sb = sb("id_sb", [P, P])
        ones = sb("ones", [P, P])
        wqk_r = [sb(f"wqk_r{i}", [P, KC, 2, 2, P], fp32r) for i in range(2)]
        bqk_sb = sb("bqk_sb", [P, 2, 2])
        wv_r = [sb(f"wv_r{i}", [P, KC, D], fp32r) for i in range(2)]
        wo_sb = sb("wo_sb", [P, KC, D])
        w1_sb = sb("w1_sb", [P, KC, F], fp32r)
        w2_sb = sb("w2_sb", [P, FT, D], fp32r)
        b1_sb = sb("b1_sb", [P, FT])
        bvc_sb = sb("bvc_sb", [P, KC])
        bo_sb = sb("bo_sb", [P, D])
        b2_sb = sb("b2_sb", [P, D])
        cs_sb = sb("cs_sb", [P, 2, 2, S])
        half_sb = sb("half_sb", [P, TL])
        asum = sb("asum", [P, 2])
        thr = sb("thr", [P, 2, 2])

        xt_sb = sb("xt_sb", [P, KC, TQ])
        xt_r = [sb(f"xt_r{i}", [P, KC, TQ], fp32r) for i in range(2)]
        ev_sb = sb("ev_sb", [P, 2, TQ])
        od_sb = sb("od_sb", [P, 2, TQ])
        os_ = sb("os_", [P, 2, TQ])
        oc = sb("oc", [P, 2, TQ])
        rot = sb("rot", [P, 2, 2, TQ])
        parts = sb("parts", [P, 2, 2, PARTS, TQ], bf16)
        v_st = sb("v_st", [P, G, TL, HG, VW])

        qa = [sb(f"qa{i}", [P, HG, S], bf16) for i in range(G)]
        ka = [sb(f"ka{i}", [P, HG, S], bf16) for i in range(G)]
        v_sb = [sb(f"v_sb{i}", [P, TT, HG, VW]) for i in range(2)]
        prob = [sb(f"prob{i}", [P, HG, NQ]) for i in range(2)]
        at_st = [sb(f"at_st{i}", [P, NQ]) for i in range(QH)]
        mxp = sb("mxp", [P, 2, HG * TT])
        mx = sb("mx", [P, HG * TT])
        nm = sb("nm", [HG * TT, MROWS, P], bf16)

        at_sb = sb("at_sb", [P, G, TQ])
        rden = sb("rden", [P, TL, H])
        att = sb("att", [P, TL, D])
        att_t = sb("att_t", [P, KC, TQ])
        xn = sb("xn", [P, TL, D])
        xb = sb("xb", [P, TL, D])
        y = sb("y", [P, TL, D])
        st = sb("st", [P, TL, 6])
        mv = sb("mv", [P, TL, 2])
        ve = sb("ve", [P, TL])
        rstd = sb("rstd", [P, TL])
        h1 = sb("h1", [P, TL, D])
        h1b = sb("h1b", [P, TL, D])
        h1_t = [sb(f"h1_t{i}", [P, KC * TQ], fp32r) for i in range(2)]
        hid = [sb(f"hid{i}", [P, TQ]) for i in range(2)]
        hid_r = [sb(f"hid_r{i}", [P, FT, TQ], fp32r) for i in range(2)]
        y2 = sb("y2", [P, TL, D])
        st2 = sb("st2", [P, TL, 6])
        mv2 = sb("mv2", [P, TL, 2])
        ve2 = sb("ve2", [P, TL])
        rstd2 = sb("rstd2", [P, TL])
        wqk_raw = at_sb[:, :, :].rearrange("p g t -> p (g t)")
        wv_raw = att[:, :, :].rearrange("p t f -> p (t f)")

        sc = [pb(f"sc{i}", [P, 2, NQ]) for i in range(2)]
        ms = [pb(f"ms{i}", [P, 512]) for i in range(2)]
        ob = pb("ob", [P, NQ])
        job = pb("job", [P, 512])

        names = """weights_loaded weights_high weights_low xt_high xt_low rope_loaded bias_spread bias_ready
            bias_folded consts_loaded w1_loaded w2_loaded abs_summed sums_ready thresholds_set thr_half
            signs_done ternary_done ones_set rows_set powers_set xt_loaded even_ready even_taken odd_ready
            odd_taken v_ready v_taken roped products rest_done mid_done parts_done parts_stored v_stored
            m_stored m_loaded s1_ready s1_taken max_done mx_ready high_done mx_taken s2_ready exp_done
            pv_done o_taken ob_zero at_loaded t1_ready recip_done t1_taken t2_ready t2_taken t3_ready
            t3_taken stats_done moments_done var_done rstd_done h1_done t4_ready t4_taken f_ready f_taken
            hid_high hid_low t4_high t6_ready t6_taken xn_loaded xb_done h1b_done stats2_done moments2_done
            var2_done rstd2_done centred res_done out_stored""".split()
        s = {n: sem(n) for n in names}
        qk_loaded = [sem(f"qk_loaded{i}") for i in range(G)]
        v_loaded = [sem(f"v_loaded{i}") for i in range(2)]
        at_stored = [sem(f"at_stored{i}") for i in range(QH)]

        def upto(b, g, each, n):
            return b * (G * each) + (g * each + n)

        block = ctx.enter_context(nc.Block())
        QK_DMAS = 2 * TERMS

        def bank_of(name, end):
            if end and name[0] == "f":
                pair = int(name[1]) // 2 % 2
                return f"sc{pair}", sc[pair][:, 0, :]
            if end and name[0] == "g":
                return "ms0", ms[0][:, :]
            return "job", job[:, :]

        def rotate(wait, engine, b, g):
            tt = engine.tensor_tensor
            cos = cs_sb[:, 0, :, g * TQ:(g + 1) * TQ]
            sin = cs_sb[:, 1, :, g * TQ:(g + 1) * TQ]
            wait_used(wait, s["roped"], upto(b, g, 2, 0))
            wait_used(wait, s["parts_done"], upto(b, g, 1, 0))
            wait.wait_ge(s["even_taken"], upto(b, g, 1, 1))
            tt(rot[:, :, 0, :], ev_sb[:, :, :], cos, ALU.mult).then_inc(s["products"], 1)
            tt(rot[:, :, 1, :], ev_sb[:, :, :], sin, ALU.mult).then_inc(s["products"], 1)
            wait.wait_ge(s["odd_taken"], upto(b, g, 1, 1))
            tt(os_[:, :, :], od_sb[:, :, :], sin, ALU.mult).then_inc(s["products"], 1)
            tt(oc[:, :, :], od_sb[:, :, :], cos, ALU.mult).then_inc(s["products"], 1)
            wait.wait_ge(s["products"], upto(b, g, 4, 4))
            wait_used(wait, s["parts_stored"], upto(b, g, 32, 0))
            tt(parts[:, :, 0, 0, :], rot[:, :, 0, :], os_[:, :, :], ALU.subtract)
            tt(parts[:, :, 1, 0, :], rot[:, :, 1, :], oc[:, :, :], ALU.add)
            tt(rot[:, :, 0, :], rot[:, :, 0, :], os_[:, :, :], ALU.subtract).then_inc(s["roped"], 1)
            tt(rot[:, :, 1, :], rot[:, :, 1, :], oc[:, :, :], ALU.add).then_inc(s["roped"], 1)

        def split(wait, engine, b, g):
            tt = engine.tensor_tensor
            wait.wait_ge(s["roped"], upto(b, g, 2, 2))
            tt(parts[:, :, :, 1, :], rot[:, :, :, :], parts[:, :, :, 0, :], ALU.subtract).then_inc(s["mid_done"], 1)
            tt(rot[:, :, :, :], rot[:, :, :, :], parts[:, :, :, 0, :], ALU.subtract).then_inc(s["rest_done"], 1)
            wait.wait_ge(s["rest_done"], upto(b, g, 1, 1))
            wait.wait_ge(s["mid_done"], upto(b, g, 1, 1))
            tt(parts[:, :, :, 2, :], rot[:, :, :, :], parts[:, :, :, 1, :], ALU.subtract).then_inc(s["parts_done"], 1)

        @block.sync
        def _(sp):
            def proj_in(b, g):
                wait_used(sp, s["xt_low"], upto(b, g, 1, 0))
                sp.dma_start(xt_sb[:, :, :], xt[b].rearrange("(c p) t -> p c t", p=P)[:, :, g * TQ:(g + 1) * TQ]
                             ).then_inc(s["xt_loaded"], 16)

            def proj_out(b, g):
                sp.wait_ge(s["v_taken"], upto(b, g, 1, 1))
                sp.dma_start(v_d[b].rearrange("g p n -> p g n")[:, :, g * TL * HG * VW:(g + 1) * TL * HG * VW],
                             v_st[:, :, :, :, :].rearrange("p g t h c -> p g (t h c)")).then_inc(s["v_stored"], 16)
                sp.wait_ge(s["parts_done"], upto(b, g, 1, 1))
                for i in range(2):
                    sp.dma_start(
                        qk_d[b, i].rearrange("(p e) a t -> p (e a) t", e=2)[:, :, g * TQ:(g + 1) * TQ],
                        parts[:, i].rearrange("p e a t -> p (e a) t")).then_inc(s["parts_stored"], 16)

            def load_qk(b, g):
                if g == 0:
                    sp.wait_ge(s["v_stored"], upto(b, G, 16, 0))
                    sp.wait_ge(s["parts_stored"], upto(b, G, 32, 0))
                for i, dst, order in ((1, ka[g], K_PARTS), (0, qa[g], Q_PARTS)):
                    rows = qk_d[b, i, g * HG * HD:(g + 1) * HG * HD].rearrange("(h r) a t -> a r h t", r=HD)
                    for n, a in enumerate(order):
                        sp.dma_start(dst[n * HD:(n + 1) * HD, :, :], rows[a]).then_inc(qk_loaded[g], 16)

            def load_v(b, g):
                sp.dma_start(v_sb[g % 2][:, :, :, :].rearrange("p t h c -> p (t h c)"), v_d[b, g]
                             ).then_inc(v_loaded[g % 2], 16)

            def move_maxima(b, g):
                sp.wait_ge(s["mx_taken"], upto(b, g, 1, 1))
                sp.dma_start(m_d[b, g].rearrange("m (r c) -> r m c", c=P), nm[:, :, :]).then_inc(s["m_stored"], 16)
                sp.wait_ge(s["m_stored"], upto(b, g, 16, 16))
                sp.dma_start(qa[g][ROWS:ROWS + MROWS, :, :].rearrange("p h t -> p (h t)"), m_d[b, g]
                             ).then_inc(s["m_loaded"], 16)

            def store_attention(b, g, qh):
                sp.wait_ge(s["o_taken"], upto(b, g, QH, qh + 1))
                sp.dma_start(at_d[b, g, :, qh * NQ:(qh + 1) * NQ], at_st[qh][:, :]).then_inc(at_stored[qh], 16)

            def tail_in(b, g):
                wait_used(sp, s["xb_done"], upto(b, g, 1, 0))
                if g == 0:
                    for qh in range(QH):
                        sp.wait_ge(at_stored[qh], upto(b, G, 16, 0))
                    wait_used(sp, s["t1_ready"], upto(b, g, TL, 0))
                sp.dma_start(xn[:, :, :], x[b, g * TQ:(g + 1) * TQ].rearrange("(t p) f -> p t f", p=P)
                             ).then_inc(s["xn_loaded"], 16)
                if g > 0:
                    wait_used(sp, s["t1_ready"], upto(b, g, TL, 0))
                sp.dma_start(at_sb[:, :, :], at_d[b].rearrange("g p t -> p g t")[:, :, g * TQ:(g + 1) * TQ]
                             ).then_inc(s["at_loaded"], 16)

            def tail_out(b, g):
                sp.wait_ge(s["res_done"], upto(b, g, 1, 1))
                sp.dma_start(out[b, g * TQ:(g + 1) * TQ].rearrange("(t p) f -> p t f", p=P), y2[:, :, :]
                             ).then_inc(s["out_stored"], 16)

            def unit(b, g, tail, last, first, tail_before):
                proj = projected(b, g)
                if len(proj) > 1:
                    proj_in(*proj[1])
                if not (first and g == 0):
                    store_attention(b + (g - 1) // G, (g - 1) % G, 1)
                if tail:
                    tail_in(b - 1, g)
                if not (last and g >= 2):
                    load_qk(b + (g + 2) // G, (g + 2) % G)
                if not (last and g == G - 1):
                    load_v(b + (g + 1) // G, (g + 1) % G)
                if tail if g else tail_before:
                    tail_out(b - 1 + (g - 1) // G, (g - 1) % G)
                if proj:
                    proj_out(*proj[0])
                for at in projected_next(b, g):
                    proj_in(*at)
                if not (last and g == G - 1):
                    move_maxima(b + (g + 1) // G, (g + 1) % G)
                store_attention(b, g, 0)
                if len(proj) > 1:
                    proj_out(*proj[1])

            def batch(b, tail=True, last=False, first=False, tail_before=True):
                for g in range(G):
                    unit(b, g, tail, last, first, tail_before)

            proj_in(0, 0)
            sp.dma_start(wqk_raw.rearrange("p (c i e m) -> p c i e m", c=KC, i=2, e=2), wqk).then_inc(s["weights_loaded"], 16)
            sp.dma_start(bqk_sb[:, :, :], bqk).then_inc(s["weights_loaded"], 16)
            sp.dma_start(wv_raw.rearrange("p (c f) -> p c f", c=KC), wv.rearrange("(c p) f -> p c f", p=P)
                         ).then_inc(s["weights_loaded"], 16)
            sp.dma_start(cs_sb[:, :, :, :], rope).then_inc(s["rope_loaded"], 16)
            sp.dma_start(prob[0][:, :, :].rearrange("p h q -> p (h q)").rearrange("p (c f) -> p c f", c=KC),
                         w1.rearrange("(c p) f -> p c f", p=P)).then_inc(s["w1_loaded"], 16)
            sp.dma_start(prob[1][:, :, :].rearrange("p h q -> p (h q)").rearrange("p (c f) -> p c f", c=FT),
                         w2.rearrange("(c p) f -> p c f", p=P)).then_inc(s["w2_loaded"], 16)
            sp.dma_start(id_sb[:, :], ident).then_inc(s["consts_loaded"], 16)
            sp.dma_start(wo_sb[:, :, :], wo.rearrange("(c p) f -> p c f", p=P)).then_inc(s["consts_loaded"], 16)
            sp.dma_start(bo_sb[:, :], bo.partition_broadcast(P)).then_inc(s["consts_loaded"], 16)
            sp.dma_start(b2_sb[:, :], b2.partition_broadcast(P)).then_inc(s["consts_loaded"], 16)
            sp.dma_start(b1_sb[:, :], b1).then_inc(s["consts_loaded"], 16)
            sp.dma_start(bvc_sb[:, :], bvc).then_inc(s["consts_loaded"], 16)
            for g in range(G):
                proj_in((g + 1) // G, (g + 1) % G)
                proj_out(0, g)
            sp.wait_ge(s["abs_summed"], 2)
            load_qk(0, 0)
            load_qk(0, 1)
            load_v(0, 0)
            move_maxima(0, 0)
            batch(0, tail=False, first=True, tail_before=False)
            batch(1, tail_before=False)
            with sp.Fori(2, B - 2) as b:
                batch(b)
            batch(B - 2)
            batch(B - 1, last=True)
            store_attention(B - 1, G - 1, 1)
            tail_in(B - 1, 0)
            tail_out(B - 2, G - 1)
            tail_in(B - 1, 1)
            for g in range(G):
                if g + 2 < G:
                    tail_in(B - 1, g + 2)
                tail_out(B - 1, g)
            sp.wait_ge(s["out_stored"], 16 * B * G)

        @block.tensor
        def _(pe):
            def proj_piece(b, g, name, bank_free):
                kind, i = name[0], int(name[1])
                if name == "e0":
                    pe.wait_ge(s["xt_low"], upto(b, g, 1, 1))
                if i == 0:
                    for what, n in bank_free:
                        wait_used(pe, s[what], n)
                terms = [(c, wp, xp) for c in range(KC) for wp, xp in ((0, 0), (1, 0), (0, 1))]
                for n, (c, wp, xp) in enumerate(terms):
                    ends = {"start": n == 0, "stop": n == len(terms) - 1}
                    if kind == "v":
                        last = nc.tensor.matmul(job[:, i * D:(i + 1) * D], xt_r[xp][:, c, i * P:(i + 1) * P],
                                                wv_r[wp][:, c, :], **ends)
                    else:
                        last = nc.tensor.matmul(job[:, i * TQ:(i + 1) * TQ], wqk_r[wp][:, c, i, "eo".index(kind), :],
                                                xt_r[xp][:, c, :], **ends)
                full = {"e": "even", "o": "odd", "v": "v"}[kind]
                if i == 1:
                    last.then_inc(s[full + "_ready"], 1)
                return [(full + "_taken", upto(b, g, 1, 1))]

            def tail_piece(b, g, name, bank_free, end=False):
                bank = bank_of(name, end)[1]
                if name == "t1a":
                    pe.wait_ge(s["at_loaded"], upto(b, g, 16, 16))
                elif name == "t2":
                    pe.wait_ge(s["t1_taken"], upto(b, g, TL, TL))
                elif name == "t3a":
                    pe.wait_ge(s["t2_taken"], upto(b, g, 1, 1))
                elif name == "t4":
                    pe.wait_ge(s["h1_done"], upto(b, g, TL, TL))
                elif name == "f0":
                    pe.wait_ge(s["t4_taken"], upto(b, g, 1, 1))
                if name in ("t1a", "t1b", "t2", "t3a", "t4", "f0", "f2", "f4", "f6", "g0"):
                    for what, n in bank_free:
                        wait_used(pe, s[what], n)
                if name in ("t1a", "t1b"):
                    tl = "ab".index(name[-1])
                    for gg in range(G):
                        last = nc.tensor.transpose(bank[:, gg * P:(gg + 1) * P], at_sb[:, gg, tl * P:(tl + 1) * P],
                                                   id_sb[:, :])
                    last.then_inc(s["t1_ready"], 1)
                    return [("t1_taken", upto(b, g, TL, tl + 1))]
                if name in ("t2", "t4"):
                    src = {"t2": att, "t4": h1}[name]
                    for c in range(KC):
                        for tl in range(TL):
                            last = nc.tensor.transpose(bank[:, c * TQ + tl * P:c * TQ + (tl + 1) * P],
                                                       src[:, tl, c * P:(c + 1) * P], id_sb[:, :])
                    last.then_inc(s[name + "_ready"], 1)
                    return [(name + "_taken", upto(b, g, 1, 1))]
                if name in ("t3a", "t3b"):
                    tl = "ab".index(name[-1])
                    for c in range(KC):
                        last = nc.tensor.matmul(bank[:, tl * D:(tl + 1) * D], att_t[:, c, tl * P:(tl + 1) * P],
                                                wo_sb[:, c, :], start=(c == 0), stop=(c == KC - 1))
                    if tl == TL - 1:
                        last.then_inc(s["t3_ready"], 1)
                    return [("t3_taken", upto(b, g, TL, TL))]
                n = int(name[1])
                if name[0] == "f":
                    for c in range(KC):
                        for part in range(2):
                            last = nc.tensor.matmul(
                                bank[:, n % 2 * TQ:(n % 2 + 1) * TQ], w1_sb[:, c, n * P:(n + 1) * P],
                                h1_t[part][:, c * TQ:(c + 1) * TQ],
                                start=(c == 0 and part == 0), stop=(c == KC - 1 and part == 1))
                    if n % 2:
                        last.then_inc(s["f_ready"], 1)
                    return [("f_taken", upto(b, g, FT, n + 1))]
                tl = n // 4
                for f in range(2 * (n % 4), 2 * (n % 4) + 2):
                    if tl == 0:
                        pe.wait_ge(s["hid_low"], upto(b, g, FT, f + 1))
                    for part in range(2):
                        last = nc.tensor.matmul(bank[:, tl * D:(tl + 1) * D], hid_r[part][:, f, tl * P:(tl + 1) * P],
                                                w2_sb[:, f, :], start=(f == 0 and part == 0),
                                                stop=(f == FT - 1 and part == 1))
                if n == 7:
                    last.then_inc(s["t6_ready"], 1)
                return [("t6_taken", upto(b, g, TL, TL))]

            def maximum(b, g, tiles):
                for n in tiles:
                    j, qt, kh = n // (2 * TT), n // 2 % TT, n % 2
                    if n == 0:
                        pe.wait_ge(qk_loaded[g], b * (16 * QK_DMAS) + 16 * QK_DMAS)
                    if not (isinstance(b, int) and upto(b, g, NS1, n) < 2):
                        pe.wait_ge(s["s1_taken"], upto(b, g, NS1, n - 1))
                    nc.tensor.matmul(ms[n % 2][:, :], qa[g][0:ROWS, j, qt * P:(qt + 1) * P],
                                     ka[g][0:ROWS, j, kh * 512:(kh + 1) * 512], start=True, stop=True
                                     ).then_inc(s["s1_ready"], 1)

            def transpose_maxima(b, g, name, bank_free):
                for what, n in bank_free:
                    wait_used(pe, s[what], n)
                pe.wait_ge(s["max_done"], upto(b, g, 1, 1))
                nc.tensor.transpose(job[0:HG * TT, 0:P], mx[:, :], id_sb[:, :]).then_inc(s["mx_ready"], 1)
                return [("mx_taken", upto(b, g, 1, 1))]

            def scores(b, g, st_, pair, first):
                qh, tt = st_ // TT, st_ % TT
                if st_ == 0 and pair == 0:
                    pe.wait_ge(s["m_loaded"], upto(b, g, 16, 16))
                if not (first and g == 0 and st_ == 0):
                    pe.wait_ge(s["exp_done"], upto(b, g, 2 * STEPS, 2 * st_ + pair - 1))
                for i in range(2):
                    j = 2 * pair + i
                    last = nc.tensor.matmul(sc[pair][:, i, :], ka[g][0:ROWS + MROWS, j, tt * P:(tt + 1) * P],
                                            qa[g][0:ROWS + MROWS, j, qh * NQ:(qh + 1) * NQ], start=True, stop=True)
                last.then_inc(s["s2_ready"], 1)

            def weigh(b, g, st_):
                qh, tt = st_ // TT, st_ % TT
                if st_ == 0:
                    pe.wait_ge(v_loaded[g % 2], b * 32 + (g // 2 + 1) * 16)
                    if isinstance(b, int) and b == 0 and g == 0:
                        pe.wait_ge(s["ob_zero"], 1)
                pe.wait_ge(s["exp_done"], upto(b, g, 2 * STEPS, 2 * st_ + 2))
                if tt == 0:
                    wait_used(pe, s["o_taken"], upto(b, g, QH, qh))
                for j in range(HG):
                    last = nc.tensor.matmul(ob[32 * j:32 * j + VW, :], v_sb[g % 2][:, tt, j, :], prob[st_ % 2][:, j, :],
                                            start=(tt == 0), stop=(tt == TT - 1))
                last.then_inc(s["pv_done"], 1)

            def run(jobs, free):
                for stage, at, name in jobs:
                    piece = {"mx": transpose_maxima, "proj": proj_piece, "tail": tail_piece}[stage]
                    free = piece(*at, name, free)
                return free

            def batch(b, tail=True, last=False, first=False):
                free = [("mx_taken", upto(b, 0, 1, 1))] + ([("t6_taken", upto(b, 0, TL, -G * TL))] if tail else [])
                for g in range(G):
                    nxt = not (last and g == G - 1)
                    for st_ in range(STEPS):
                        jobs = [pieces(b, g, 2 * st_ + half, tail, nxt) for half in range(2)]
                        tiles = [maximum_tiles(b, g, 4 * st_ + n, last) for n in range(4)]
                        scores(b, g, st_, 0, first)
                        maximum(*tiles[0])
                        if jobs[0]:
                            free = run(jobs[0], free)
                            maximum(*tiles[1])
                            scores(b, g, st_, 1, first)
                        else:
                            scores(b, g, st_, 1, first)
                            maximum(*tiles[1])
                        free = run(jobs[1], free)
                        maximum(*tiles[2])
                        if st_ > 0:
                            weigh(b, g, st_ - 1)
                        elif not (first and g == 0):
                            weigh(b + (g - 1) // G, (g - 1) % G, STEPS - 1)
                        maximum(*tiles[3])

            pe.wait_ge(s["ones_set"], 1)
            pe.wait_ge(s["weights_low"], 2)
            free = []
            for g in range(G):
                for name in ("e0", "e1", "o0", "o1", "v0", "v1"):
                    free = proj_piece(0, g, name, free)
            pe.wait_ge(s["v_taken"], G)
            pe.wait_ge(s["abs_summed"], 2)
            nc.tensor.matmul(job[:, 0:2], ones[:, :], asum[:, :], start=True, stop=True).then_inc(s["sums_ready"], 1)
            pe.wait_ge(qk_loaded[0], 16 * QK_DMAS)
            for n in range(NS1 // 2):
                if n >= 2:
                    pe.wait_ge(s["s1_taken"], 2 * (n - 1))
                for kh in range(2):
                    nc.tensor.matmul(sc[n % 2][:, kh, :], qa[0][0:ROWS, n // TT, n % TT * P:(n % TT + 1) * P],
                                     ka[0][0:ROWS, n // TT, kh * 512:(kh + 1) * 512], start=True, stop=True
                                     ).then_inc(s["s1_ready"], 1)
            pe.wait_ge(s["s1_taken"], NS1)
            pe.wait_ge(s["consts_loaded"], 96)
            pe.wait_ge(s["bias_spread"], KC)
            pe.wait_ge(s["thr_half"], 1)
            for c in range(KC):
                last = nc.tensor.matmul(job[:, 0:D], y2[:, c, 0:P], wo_sb[:, c, :], start=(c == 0), stop=(c == KC - 1))
            last.then_inc(s["bias_ready"], 1)
            transpose_maxima(0, 0, "mx", [("bias_folded", 1)])
            pe.wait_ge(s["ternary_done"], 2)
            pe.wait_ge(s["rows_set"], G)
            batch(0, tail=False, first=True)
            batch(1)
            with pe.Fori(2, B - 2) as b:
                batch(b)
            batch(B - 2)
            batch(B - 1, last=True)
            weigh(B - 1, G - 1, STEPS - 1)
            pe.wait_ge(s["exp_done"], B * G * 2 * STEPS)
            pe.wait_ge(s["s1_taken"], B * G * NS1)
            frees = {"job": [("t6_taken", upto(B - 1, 0, TL, 0))]}
            for kind, g, name in end_steps():
                if name[0] in "tfg" and name[1].isdigit():
                    bank = bank_of(name, True)[0]
                    frees[bank] = tail_piece(B - 1, g, name, frees.get(bank, []), True)

        @block.scalar
        def _(act):
            def exps(b, g, st_, pair):
                act.wait_ge(s["s2_ready"], upto(b, g, 2 * STEPS, 2 * st_ + pair + 1))
                if pair == 0 and not (isinstance(b, int) and b == 0 and g == 0 and st_ < 2):
                    act.wait_ge(s["pv_done"], upto(b, g, STEPS, st_ - 1))
                nc.scalar.activation(prob[st_ % 2][:, 2 * pair:2 * pair + 2, :], sc[pair][:, :, :], ACT.Exp
                                     ).then_inc(s["exp_done"], 1)

            def take_outputs(b, g, qh):
                act.wait_ge(s["pv_done"], upto(b, g, STEPS, (qh + 1) * TT))
                wait_used(act, at_stored[qh], upto(b, g, 16, 0))
                nc.scalar.activation(at_st[qh][:, :], ob[:, :], ACT.Copy).then_inc(s["o_taken"], 1)

            def split_x(b, g):
                act.wait_ge(s["xt_loaded"], upto(b, g, 16, 16))
                wait_used(act, s["v_ready"], upto(b, g, 1, 0))
                nc.scalar.activation(xt_r[0][:, :, :], xt_sb[:, :, :], ACT.Copy).then_inc(s["xt_high"], 1)

            def proj_piece(b, g, name):
                if name == "v1":
                    act.wait_ge(s["v_ready"], upto(b, g, 1, 1))
                    wait_used(act, s["v_stored"], upto(b, g, 16, 0))
                    for tl in range(TL):
                        done = nc.scalar.activation(
                            v_st[:, :, tl, :, 0:HD],
                            job[:, tl * D:(tl + 1) * D].rearrange("p (g h c) -> p g h c", g=G, h=HG), ACT.Copy)
                    done.then_inc(s["v_taken"], 1)
                if name not in ("e1", "o1"):
                    return
                eo = "eo".index(name[0])
                full = ("even", "odd")[eo]
                act.wait_ge(s[full + "_ready"], upto(b, g, 1, 1))
                wait_used(act, s["products"], upto(b, g, 4, 0))
                for i in range(2):
                    done = nc.scalar.activation((ev_sb, od_sb)[eo][:, i, :], job[:, i * TQ:(i + 1) * TQ], ACT.Identity,
                                                bias=bqk_sb[:, i, eo:eo + 1])
                done.then_inc(s[full + "_taken"], 1)

            def tail_piece(b, g, name, end=False):
                bank = bank_of(name, end)[1]
                if name == "t2":
                    act.wait_ge(s["t2_ready"], upto(b, g, 1, 1))
                    nc.scalar.activation(att_t[:, :, :].rearrange("p c t -> p (c t)"), bank[:, :], ACT.Copy
                                         ).then_inc(s["t2_taken"], 1)
                if name == "t4":
                    act.wait_ge(s["t4_ready"], upto(b, g, 1, 1))
                    nc.scalar.activation(h1_t[0][:, :], bank[:, :], ACT.Copy).then_inc(s["t4_high"], 1)
                if name in ("f1", "f3", "f5", "f7"):
                    n = int(name[1])
                    act.wait_ge(s["f_ready"], upto(b, g, FT // 2, n // 2 + 1))
                    for i in range(2):
                        f = n - 1 + i
                        src, bias = bank[:, i * TQ:(i + 1) * TQ], b1_sb[:, f:f + 1]
                        nc.scalar.activation(hid_r[0][:, f, :], src, ACT.Relu, bias=bias).then_inc(s["hid_high"], 1)
                        wait_used(act, s["hid_low"], upto(b, g, FT, f - 1))
                        nc.scalar.activation(hid[i][:, :], src, ACT.Relu, bias=bias).then_inc(s["f_taken"], 1)

            def batch(b, tail=True, first=False):
                for g in range(G):
                    for st_ in range(STEPS):
                        for half in range(2):
                            exps(b, g, st_, half)
                            if st_ == TT + 1 and half == 0:
                                take_outputs(b, g, 0)
                            if st_ == 1 and half == 0 and not (first and g == 0):
                                take_outputs(b + (g - 1) // G, (g - 1) % G, 1)
                            for stage, at, name in pieces(b, g, 2 * st_ + half, tail, False):
                                {"proj": proj_piece, "tail": tail_piece}[stage](*at, name)
                            if 2 * st_ + half == SECOND_SPLIT_SLOT:
                                for at in projected(b, g)[1:]:
                                    split_x(*at)
                            if 2 * st_ + half == SPLIT_SLOT:
                                for at in projected_next(b, g):
                                    split_x(*at)

            act.wait_ge(s["weights_loaded"], 48)
            for w, raw in ((wqk_r, wqk_raw), (wv_r, wv_raw)):
                high = w[0][:, :, :, :, :].rearrange("p c i e m -> p (c i e m)") if w is wqk_r else (
                    w[0][:, :, :].rearrange("p c f -> p (c f)"))
                nc.scalar.activation(high, raw, ACT.Copy).then_inc(s["weights_high"], 1)
            split_x(0, 0)
            act.wait_ge(s["ones_set"], 1)
            for g in range(G):
                for name in ("e1", "o1", "v1"):
                    proj_piece(0, g, name)
                split_x((g + 1) // G, (g + 1) % G)
                if g < 2:
                    act.wait_ge(s[("w1_loaded", "w2_loaded")[g]], 16)
                    nc.scalar.activation(qa[g][:, 0:2, :].rearrange("p h q -> p (h q)"),
                                         prob[g][:, :, :].rearrange("p h q -> p (h q)"),
                                         ACT.Abs, accum_out=asum[:, g:g + 1]).then_inc(s["abs_summed"], 1)
            act.wait_ge(s["consts_loaded"], 96)
            act.wait_ge(s["ternary_done"], 2)
            batch(0, tail=False, first=True)
            batch(1)
            with act.Fori(2, B - 2) as b:
                batch(b)
            batch(B - 2)
            batch(B - 1)
            take_outputs(B - 1, G - 1, 1)
            for kind, g, name in end_steps():
                tail_piece(B - 1, g, name, True)

        @block.vector
        def _(dve):
            def maximum(b, g, tiles):
                for n in tiles:
                    if n == 0:
                        wait_used(dve, s["max_done"], upto(b, g, 1, 0))
                    dve.wait_ge(s["s1_ready"], upto(b, g, NS1, n + 1))
                    nc.vector.reduce_max(mxp[:, n % 2, n // 2:n // 2 + 1], ms[n % 2][:, :], AX.X
                                         ).then_inc(s["s1_taken"], 1)

            def combine(b, g):
                dve.wait_ge(s["s1_taken"], upto(b, g, NS1, NS1))
                wait_used(dve, s["mx_ready"], upto(b, g, 1, 0))
                nc.vector.tensor_tensor(mx[:, :], mxp[:, 0, :], mxp[:, 1, :], ALU.max).then_inc(s["max_done"], 1)

            def take_maxima(b, g):
                dve.wait_ge(s["mx_ready"], upto(b, g, 1, 1))
                wait_used(dve, s["m_stored"], upto(b, g, 16, 0))
                nc.vector.tensor_scalar(nm[:, 0, :], job[0:HG * TT, 0:P], -1.0, None, ALU.mult
                                        ).then_inc(s["high_done"], 1)

            def take_low_maxima(b, g):
                dve.wait_ge(s["high_done"], upto(b, g, 1, 1))
                nc.vector.scalar_tensor_tensor(out=nm[:, 1, :], in0=job[0:HG * TT, 0:P], scalar=-1.0, in1=nm[:, 0, :],
                                               op0=ALU.mult, op1=ALU.subtract).then_inc(s["mx_taken"], 1)

            def statistics(b, g, tl, src_done, src, stats, tag):
                dve.wait_ge(s[src_done], upto(b, g, TL, tl + 1))
                if tl:
                    dve.wait_ge(s["stats" + tag], upto(b, g, TL, tl))
                nc.vector.bn_stats(stats[:, tl, :], src[:, tl, :]).then_inc(s["stats" + tag], 1)

            def moments_of(b, g, stats, moments, var, tag):
                nc.vector.bn_aggr(moments[:, 0, :], stats[:, 0, :]).then_inc(s["moments" + tag], 1)
                dve.wait_ge(s["moments" + tag], upto(b, g, TL, 1))
                dve.wait_ge(s["stats" + tag], upto(b, g, TL, 2))
                nc.vector.tensor_scalar(var[:, 0:1], moments[:, 0, 1:2], EPS, None, ALU.add).then_inc(s["var" + tag], 1)
                nc.vector.bn_aggr(moments[:, 1, :], stats[:, 1, :]).then_inc(s["moments" + tag], 1)
                dve.wait_ge(s["moments" + tag], upto(b, g, TL, 2))
                nc.vector.tensor_scalar(var[:, 1:2], moments[:, 1, 1:2], EPS, None, ALU.add).then_inc(s["var" + tag], 1)

            def tail_piece(b, g, name):
                if name in ("t1a", "t1b"):
                    tl = "ab".index(name[-1])
                    dve.wait_ge(s["t1_ready"], upto(b, g, TL, tl + 1))
                    heads = job[:, :].rearrange("p (h c) -> p h c", c=32)
                    nc.vector.reciprocal(rden[:, tl, :], heads[:, :, HD]).then_inc(s["recip_done"], 1)
                    dve.wait_ge(s["recip_done"], upto(b, g, TL, tl + 1))
                    nc.vector.tensor_tensor(att[:, tl, :].rearrange("p (h c) -> p h c", c=HD), heads[:, :, 0:HD],
                                            rden[:, tl, :].unsqueeze(2).broadcast_to([P, H, HD]), ALU.mult
                                            ).then_inc(s["t1_taken"], 1)
                elif name == "t4":
                    dve.wait_ge(s["t4_high"], upto(b, g, 1, 1))
                    nc.vector.tensor_tensor(h1_t[1][:, :], job[:, :], h1_t[0][:, :], ALU.subtract
                                            ).then_inc(s["t4_taken"], 1)

            def add_residual(b, g, tl, product, other_done, other, dst, bank):
                dve.wait_ge(s[product + "_ready"], upto(b, g, 1, 1))
                dve.wait_ge(s[other_done], upto(b, g, 1, 1))
                nc.vector.tensor_tensor(dst[:, tl, :], bank[:, tl * D:(tl + 1) * D], other[:, tl, :], ALU.add
                                        ).then_inc(s[product + "_taken"], 1)

            def first_norm(b, g, step):
                if step is None:
                    return
                kind, tl = step.split()[0], int(step.split()[-1])
                if kind == "sum":
                    add_residual(b, g, tl, "t3", "xb_done", xb, y, job)
                elif kind == "stats":
                    statistics(b, g, tl, "t3_taken", y, st, "_done")
                elif kind == "moments":
                    moments_of(b, g, st, mv, ve, "_done")
                else:
                    if tl == 0:
                        dve.wait_ge(s["rstd_done"], upto(b, g, 1, 1))
                    nc.vector.tensor_scalar(h1[:, tl, :], y[:, tl, :], mv[:, tl, 0:1], rstd[:, tl:tl + 1],
                                            ALU.subtract, ALU.mult).then_inc(s["h1_done"], 1)

            def second_norm(b, g, step, end=False):
                if step is None:
                    return
                kind, tl = step.split()[0], int(step.split()[-1])
                if kind == "sum":
                    wait_used(dve, s["out_stored"], upto(b, g, 16, 0))
                    add_residual(b, g, tl, "t6", "h1b_done", h1b, y2, bank_of("g7", end)[1])
                elif kind == "stats":
                    statistics(b, g, tl, "t6_taken", y2, st2, "2_done")
                else:
                    moments_of(b, g, st2, mv2, ve2, "2_done")

            def batch(b, tail=True, last=False, tail_before=True):
                for g in range(G):
                    nxt = not (last and g == G - 1)
                    before = b - 1 + (g - 1) // G, (g - 1) % G
                    for slot in range(2 * STEPS):
                        for part in range(2):
                            maximum(*maximum_tiles(b, g, 2 * slot + part, last))
                            if part and nxt and slot == 2 * (STEPS - MAX_AHEAD) - 1:
                                combine(b + (g + 1) // G, (g + 1) % G)
                            if tail if g else tail_before:
                                second_norm(*before, SECOND_NORM.get((slot, part)))
                            if tail:
                                first_norm(b - 1, g, FIRST_NORM.get((slot, part)))
                            if nxt and (slot, part) == LOW_MAXIMA_AT:
                                take_low_maxima(b + (g + 1) // G, (g + 1) % G)
                        for stage, at, name in pieces(b, g, slot, tail, nxt):
                            if stage == "mx":
                                take_maxima(*at)
                            elif stage == "tail":
                                tail_piece(*at, name)

            nc.vector.memset(ob[:, :], 0.0).then_inc(s["ob_zero"], 1)
            nc.vector.memset(v_st[:, :, :, :, :].rearrange("p g t h c -> p (g t h c)"), 1.0)
            nc.vector.memset(ones[:, :], 1.0).then_inc(s["ones_set"], 1)
            for n, (w, raw) in enumerate(((wqk_r, wqk_raw), (wv_r, wv_raw))):
                high, low = (part[:, :, :, :, :].rearrange("p c i e m -> p (c i e m)") if n == 0 else
                             part[:, :, :].rearrange("p c f -> p (c f)") for part in w)
                dve.wait_ge(s["weights_high"], n + 1)
                nc.vector.tensor_tensor(low, raw, high, ALU.subtract).then_inc(s["weights_low"], 1)
            dve.wait_ge(s["ones_set"], 1)
            dve.wait_ge(s["rope_loaded"], 16)
            for g in range(G):
                rotate(dve, nc.vector, 0, g)
                split(dve, nc.vector, 0, g)
            dve.wait_ge(s["sums_ready"], 1)
            nc.vector.tensor_scalar(thr[:, 1, :], job[:, 0:2], 1.0 / (D * F), EPS, ALU.mult, ALU.add
                                    ).then_inc(s["thr_half"], 1)
            dve.wait_ge(s["thr_half"], 1)
            nc.vector.tensor_scalar(thr[:, 0, :], thr[:, 1, :], 0.5, None, ALU.mult).then_inc(s["thr_half"], 1)
            dve.wait_ge(s["thr_half"], 2)
            nc.vector.tensor_scalar(thr[:, 1, :], thr[:, 0, :], -1.0, None, ALU.mult).then_inc(s["thresholds_set"], 1)
            dve.wait_ge(s["thresholds_set"], 1)
            for i, w in enumerate((w1_sb, w2_sb)):
                raw = prob[i][:, :, :].rearrange("p h q -> p (h q)")
                below = qa[2][:, 0:2, :].rearrange("p h q -> p (h q)")
                if i:
                    dve.wait_ge(s["ternary_done"], i)
                nc.vector.tensor_scalar(below, raw, thr[:, 1, i:i + 1], None, ALU.is_lt).then_inc(s["signs_done"], 1)
                dve.wait_ge(s["signs_done"], i + 1)
                nc.vector.scalar_tensor_tensor(out=w[:, :, :].rearrange("p c f -> p (c f)"), in0=raw, scalar=thr[:, 0, i:i + 1], in1=below,
                                               op0=ALU.is_gt, op1=ALU.subtract).then_inc(s["ternary_done"], 1)
            for n in range(NS1 // 2):
                dve.wait_ge(s["s1_ready"], 2 * n + 2)
                nc.vector.reduce_max(mxp[:, 0, n:n + 1], sc[n % 2][:, :, :], AX.XY).then_inc(s["s1_taken"], 2)
            dve.wait_ge(s["s1_taken"], NS1)
            nc.vector.tensor_copy(mx[:, :], mxp[:, 0, :]).then_inc(s["max_done"], 1)
            dve.wait_ge(s["consts_loaded"], 96)
            for c in range(KC):
                nc.vector.tensor_scalar(y2[:, c, 0:P], ones[:, :], bvc_sb[:, c:c + 1], None, ALU.mult
                                        ).then_inc(s["bias_spread"], 1)
            dve.wait_ge(s["bias_ready"], 1)
            nc.vector.tensor_tensor(bo_sb[:, :], job[:, 0:D], bo_sb[:, :], ALU.add).then_inc(s["bias_folded"], 1)
            take_maxima(0, 0)
            take_low_maxima(0, 0)
            batch(0, tail=False, tail_before=False)
            batch(1, tail_before=False)
            with dve.Fori(2, B - 2) as b:
                batch(b)
            batch(B - 2)
            batch(B - 1, last=True)
            for step in SECOND_NORM.values():
                second_norm(B - 2, G - 1, step)
            for kind, g, name in end_steps():
                if kind == "after":
                    second_norm(B - 1, g, name, True)
                elif name in FIRST_NORM.values():
                    first_norm(B - 1, g, name)
                else:
                    tail_piece(B - 1, g, name)

        @block.gpsimd
        def _(pool):
            def add_bias(b, g, src_done, n, src, bias, dst, used, done):
                pool.wait_ge(s[src_done], n)
                wait_used(pool, s[used], upto(b, g, TL, 0))
                for tl in range(TL):
                    last = nc.gpsimd.tensor_tensor(dst[:, tl, :], src[:, tl, :], bias[:, :], ALU.add)
                last.then_inc(s[done], 1)

            def split_x(b, g):
                pool.wait_ge(s["xt_high"], upto(b, g, 1, 1))
                nc.gpsimd.tensor_tensor(xt_r[1][:, :, :], xt_sb[:, :, :], xt_r[0][:, :, :], ALU.subtract
                                        ).then_inc(s["xt_low"], 1)

            def sum_x(b, g):
                add_bias(b, g, "xn_loaded", upto(b, g, 16, 16), xn, bo_sb, xb, "t3_taken", "xb_done")

            def sum_h1(b, g):
                add_bias(b, g, "h1_done", upto(b, g, TL, TL), h1, b2_sb, h1b, "t6_taken", "h1b_done")

            def power(b, g, var, dst, tag):
                pool.wait_ge(s["var" + tag], upto(b, g, TL, TL))
                nc.gpsimd.tensor_tensor(dst[:, :], var[:, :], half_sb[:, :], ALU.pow).then_inc(s["rstd" + tag], 1)

            def low_parts(b, g, tiles):
                for f in tiles:
                    pool.wait_ge(s["f_taken"], upto(b, g, FT, f + 1))
                    pool.wait_ge(s["hid_high"], upto(b, g, FT, f + 1))
                    nc.gpsimd.tensor_tensor(hid_r[1][:, f, :], hid[f % 2][:, :], hid_r[0][:, f, :], ALU.subtract
                                            ).then_inc(s["hid_low"], 1)

            def finish_second_norm(b, g):
                power(b, g, ve2, rstd2, "2_done")
                pool.wait_ge(s["rstd2_done"], upto(b, g, 1, 1))
                each = [P, TL, D]
                nc.gpsimd.tensor_tensor(y2[:, :, :], y2[:, :, :], mv2[:, :, 0:1].broadcast_to(each), ALU.subtract
                                        ).then_inc(s["centred"], 1)
                pool.wait_ge(s["centred"], upto(b, g, 1, 1))
                nc.gpsimd.tensor_tensor(y2[:, :, :], y2[:, :, :], rstd2[:, :].unsqueeze(2).broadcast_to(each), ALU.mult
                                        ).then_inc(s["res_done"], 1)

            def unit(b, g, tail, tail_before):
                proj = projected(b, g)
                if tail if g else tail_before:
                    finish_second_norm(b - 1 + (g - 1) // G, (g - 1) % G)
                if tail:
                    sum_x(b - 1, g)
                for at in proj:
                    rotate(pool, nc.gpsimd, *at)
                    if at == proj[0] and len(proj) > 1:
                        split_x(*proj[1])
                    split(pool, nc.gpsimd, *at)
                if tail:
                    power(b - 1, g, ve, rstd, "_done")
                    sum_h1(b - 1, g)
                    low_parts(b - 1, g, range(FT))
                for at in projected_next(b, g):
                    split_x(*at)

            def batch(b, tail=True, tail_before=True):
                for g in range(G):
                    unit(b, g, tail, tail_before)

            nc.gpsimd.memset(half_sb[:, :], -0.5).then_inc(s["powers_set"], 1)
            for n in range(G + 1):
                split_x(n // G, n % G)
            pool.wait_ge(s["xt_low"], G + 1)
            for i in range(G):
                nc.gpsimd.memset(ka[i][ROWS:ROWS + MROWS, :, :], 1.0).then_inc(s["rows_set"], 1)
                pool.wait_ge(s["rows_set"], i + 1)
            pool.wait_ge(s["consts_loaded"], 96)
            pool.wait_ge(s["rope_loaded"], 16)
            pool.wait_ge(s["powers_set"], 1)
            pool.wait_ge(s["bias_folded"], 1)
            batch(0, tail=False, tail_before=False)
            batch(1, tail_before=False)
            with pool.Fori(2, B - 2) as b:
                batch(b)
            batch(B - 2)
            batch(B - 1)
            finish_second_norm(B - 2, G - 1)
            for g in range(G + 1):
                if g < G:
                    sum_x(B - 1, g)
                if g > 0:
                    low_parts(B - 1, g - 1, range(FT))
                if g < G:
                    power(B - 1, g, ve, rstd, "_done")
                    sum_h1(B - 1, g)
                if g > 0:
                    finish_second_norm(B - 1, g - 1)


def rope_table():
    one = np.float32(1.0)
    inv = one / np.float32(10000.0) ** (np.arange(0, HD, 2, dtype=np.float32) / np.float32(HD))
    angle = np.arange(S, dtype=np.float32)[None, :] * inv[:, None].astype(np.float32)
    table = np.stack([np.cos(angle), np.sin(angle)], axis=1)
    scale = np.array([HD ** -0.5, 1.0], np.float32)
    table = table[:, :, None, :] * scale[None, None, :, None]
    return np.ascontiguousarray(np.tile(table, (H, 1, 1, 1)).astype(np.float32))


def kernel(**inputs):
    import concourse.bacc as bacc
    from concourse.bass_utils import run_bass_kernel_spmd as run

    a = {n: np.asarray(v) for n, v in inputs.items()}

    def pairs(w):
        return np.moveaxis(w.reshape(H, HD // 2, 2, *w.shape[1:]), 2, 0).reshape(2, P, *w.shape[1:])

    wqk = np.stack([pairs(a["L0_attn_Wq"]), pairs(a["L0_attn_Wk"])])
    wqk = wqk.reshape(2, 2, P, KC, P).transpose(4, 3, 0, 1, 2)
    bqk = np.stack([pairs(a["L0_attn_bq"]), pairs(a["L0_attn_bk"])]).transpose(2, 0, 1)
    arrays = {
        "x": a["L0_attn_x"],
        "xt": a["L0_attn_x"].transpose(0, 2, 1),
        "wqk": wqk,
        "bqk": bqk,
        "wv": a["L0_attn_Wv"].T,
        "bvc": a["L0_attn_bv"].reshape(KC, P).T,
        "wo": a["L0_attn_Wo"].T,
        "bo": a["L0_attn_bo"],
        "w1": a["L0_ffn_W1"].T,
        "b1": a["L0_ffn_b1"].reshape(FT, P).T,
        "w2": a["L0_ffn_W2"].T,
        "b2": a["L0_ffn_b2"],
        "rope": rope_table(),
        "ident": np.eye(P, dtype=np.float32),
    }
    arrays = {n: np.ascontiguousarray(v) for n, v in arrays.items()}
    nc = bacc.Bacc("TRN2", target_bir_lowering=False, num_devices=1)
    args = [nc.dram_tensor(n, v.shape, mybir.dt.from_np(v.dtype), kind="ExternalInput").ap() for n, v in arrays.items()]
    args.append(nc.dram_tensor("out", (B, S, D), mybir.dt.float32, kind="ExternalOutput").ap())
    build(nc, *args)
    r = run(nc, [arrays], core_ids=[0])
    return r.results[0]["out"]
```
